# Optimizing a Trainium2 kernel written in Bass

```python
import numpy as np
import jax
import jax.numpy as jnp

def _softmax(x, axis=-1):
    return jax.nn.softmax(x, axis=axis)

def _gelu(x):
    return jax.nn.gelu(x, approximate=True)

def _silu(x):
    return jax.nn.silu(x)

def _sigmoid(x):
    return jax.nn.sigmoid(x)

def _layernorm(x, axis=-1, eps=1e-05):
    m = jnp.mean(x, axis=axis, keepdims=True)
    v = jnp.var(x, axis=axis, keepdims=True)
    return (x - m) / jnp.sqrt(v + eps)

def _scatter_add(tgt, idx, src, axis=0):
    return tgt.at[idx].add(src)

def _segment_sum(src, seg, n):
    return jax.ops.segment_sum(src, seg, n)
kernel_name = 'mk_hybrid_d1_jaxref_r4_2c368b'

def setup_inputs(seed: int=0):
    np.random.seed(seed)
    _w = jnp.asarray

    def _L0_attn_a_setup():
        import jax, jax.numpy as jnp
        import numpy as np
        EMBED_DIM = 512
        NUM_HEADS = 32
        HEAD_DIM = EMBED_DIM // NUM_HEADS
        BATCH = 2
        SEQ_LEN = 512
        key = jax.random.key(seed)
        ks = jax.random.split(key, 5)
        scale = 1.0 / np.sqrt(EMBED_DIM)
        x = jax.random.normal(ks[0], (BATCH, SEQ_LEN, EMBED_DIM), dtype=jnp.float32)
        Wq = jax.random.normal(ks[1], (EMBED_DIM, EMBED_DIM), dtype=jnp.float32) * scale
        Wk = jax.random.normal(ks[2], (EMBED_DIM, EMBED_DIM), dtype=jnp.float32) * scale
        Wv = jax.random.normal(ks[3], (EMBED_DIM, EMBED_DIM), dtype=jnp.float32) * scale
        Wo = jax.random.normal(ks[4], (EMBED_DIM, EMBED_DIM), dtype=jnp.float32) * scale
        return {'x': x, 'Wq': Wq, 'Wk': Wk, 'Wv': Wv, 'Wo': Wo}
    _L0_attn_a_in = _L0_attn_a_setup()

    def _L0_attn_b_setup():
        import jax, jax.numpy as jnp
        import numpy as np
        from jax import lax
        B, T = (2, 512)
        HID = 512
        H, K, KC = (16, 128, 4)
        D = H * K
        EPS = 1e-05
        SCALE = K ** (-0.5)

        def causal_conv_silu(x, w, b):
            xp = jnp.pad(jnp.swapaxes(x, 1, 2), ((0, 0), (0, 0), (KC - 1, 0)))
            y = lax.conv_general_dilated(xp, w[:, None, :], (1,), 'VALID', feature_group_count=D)
            return jax.nn.silu(jnp.swapaxes(y, 1, 2) + b)

        def l2norm(x):
            return x * lax.rsqrt(jnp.sum(x * x, -1, keepdims=True) + 1e-06)

        def kda_scan(q, k, v, g, beta):
            qT, kT, vT, gT, bT = (jnp.moveaxis(a, 1, 0) for a in (q, k, v, g, beta))
            S0 = jnp.zeros((q.shape[0], H, K, K), q.dtype)

            def step(S, inp):
                qt, kt, vt, gt, bt = inp
                S = S * jnp.exp(gt)[..., None]
                vd = (vt - jnp.einsum('bhkv,bhk->bhv', S, kt)) * bt[..., None]
                S = S + kt[..., None] * vd[:, :, None, :]
                return (S, jnp.einsum('bhkv,bhk->bhv', S, qt))
            _, o = lax.scan(step, S0, (qT, kT, vT, gT, bT))
            return jnp.moveaxis(o, 0, 1)

        def _forward(x, Wq, Wk, Wv, conv_q_w, conv_q_b, conv_k_w, conv_k_b, conv_v_w, conv_v_b, Wfa, Wfb, A_log, dt_bias, Wb, Wga, Wgb, o_norm_w, Wo):
            b, t = x.shape[:2]
            q = causal_conv_silu(x @ Wq, conv_q_w, conv_q_b).reshape(b, t, H, K)
            k = causal_conv_silu(x @ Wk, conv_k_w, conv_k_b).reshape(b, t, H, K)
            v = causal_conv_silu(x @ Wv, conv_v_w, conv_v_b).reshape(b, t, H, K)
            g = jax.nn.softplus(x @ Wfa @ Wfb + dt_bias).reshape(b, t, H, K)
            g = -jnp.exp(A_log)[None, None, :, None] * g
            beta = jax.nn.sigmoid(x @ Wb)
            q = l2norm(q) * SCALE
            k = l2norm(k)
            o = kda_scan(q, k, v, g, beta)
            gate = (x @ Wga @ Wgb).reshape(b, t, H, K)
            var = jnp.mean(o * o, -1, keepdims=True)
            o = o * lax.rsqrt(var + EPS) * o_norm_w * jax.nn.sigmoid(gate)
            return o.reshape(b, t, D) @ Wo
        key = jax.random.key(seed)
        ks = jax.random.split(key, 16)
        s = 0.02
        f32 = jnp.float32
        return {'x': jax.random.normal(ks[0], (B, T, HID), f32), 'Wq': jax.random.normal(ks[1], (HID, D), f32) * s, 'Wk': jax.random.normal(ks[2], (HID, D), f32) * s, 'Wv': jax.random.normal(ks[3], (HID, D), f32) * s, 'conv_q_w': jax.random.normal(ks[4], (D, KC), f32) * 0.2, 'conv_q_b': jnp.zeros((D,), f32), 'conv_k_w': jax.random.normal(ks[5], (D, KC), f32) * 0.2, 'conv_k_b': jnp.zeros((D,), f32), 'conv_v_w': jax.random.normal(ks[6], (D, KC), f32) * 0.2, 'conv_v_b': jnp.zeros((D,), f32), 'Wfa': jax.random.normal(ks[7], (HID, K), f32) * s, 'Wfb': jax.random.normal(ks[8], (K, D), f32) * s, 'A_log': jnp.log(jax.random.uniform(ks[9], (H,), f32, 1.0, 16.0)), 'dt_bias': jnp.zeros((D,), f32), 'Wb': jax.random.normal(ks[10], (HID, H), f32) * s, 'Wga': jax.random.normal(ks[11], (HID, K), f32) * s, 'Wgb': jax.random.normal(ks[12], (K, D), f32) * s, 'o_norm_w': jnp.ones((K,), f32), 'Wo': jax.random.normal(ks[13], (D, HID), f32) * s}
    _L0_attn_b_in = _L0_attn_b_setup()

    def _L0_ffn_setup():
        import jax, jax.numpy as jnp
        import numpy as np
        B, S, D = (4, 512, 512)
        E = 8
        N_SHARE = 2
        N_ROUTED = E - N_SHARE
        H = 2048 // E
        key = jax.random.key(seed)
        ks = jax.random.split(key, 12)
        s = 0.02
        return {'x': jax.random.normal(ks[0], (B, S, D), jnp.float32), 'Wg': jax.random.normal(ks[1], (D, E), jnp.float32) * s, 'bg': jnp.zeros((E,), jnp.float32), 'Wgate': jax.random.normal(ks[2], (N_ROUTED, D, H), jnp.float32) * s, 'bgate': jnp.zeros((N_ROUTED, H), jnp.float32), 'Wup': jax.random.normal(ks[3], (N_ROUTED, D, H), jnp.float32) * s, 'bup': jnp.zeros((N_ROUTED, H), jnp.float32), 'Wdown': jax.random.normal(ks[4], (N_ROUTED, H, D), jnp.float32) * s, 'bdown': jnp.zeros((N_ROUTED, D), jnp.float32), 'Ws_up': jax.random.normal(ks[5], (D, N_SHARE * H), jnp.float32) * s, 'bs_up': jnp.zeros((N_SHARE * H,), jnp.float32), 'Ws_down': jax.random.normal(ks[6], (N_SHARE * H, D), jnp.float32) * s, 'bs_down': jnp.zeros((D,), jnp.float32)}
    _L0_ffn_in = _L0_ffn_setup()
    _d = {'L0_attn_a_x': _L0_attn_a_in['x'], 'L0_attn_a_Wq': _L0_attn_a_in['Wq'], 'L0_attn_a_Wk': _L0_attn_a_in['Wk'], 'L0_attn_a_Wv': _L0_attn_a_in['Wv'], 'L0_attn_a_Wo': _L0_attn_a_in['Wo'], 'L0_attn_b_Wq': _L0_attn_b_in['Wq'], 'L0_attn_b_Wk': _L0_attn_b_in['Wk'], 'L0_attn_b_Wv': _L0_attn_b_in['Wv'], 'L0_attn_b_conv_q_w': _L0_attn_b_in['conv_q_w'], 'L0_attn_b_conv_q_b': _L0_attn_b_in['conv_q_b'], 'L0_attn_b_conv_k_w': _L0_attn_b_in['conv_k_w'], 'L0_attn_b_conv_k_b': _L0_attn_b_in['conv_k_b'], 'L0_attn_b_conv_v_w': _L0_attn_b_in['conv_v_w'], 'L0_attn_b_conv_v_b': _L0_attn_b_in['conv_v_b'], 'L0_attn_b_Wfa': _L0_attn_b_in['Wfa'], 'L0_attn_b_Wfb': _L0_attn_b_in['Wfb'], 'L0_attn_b_A_log': _L0_attn_b_in['A_log'], 'L0_attn_b_dt_bias': _L0_attn_b_in['dt_bias'], 'L0_attn_b_Wb': _L0_attn_b_in['Wb'], 'L0_attn_b_Wga': _L0_attn_b_in['Wga'], 'L0_attn_b_Wgb': _L0_attn_b_in['Wgb'], 'L0_attn_b_o_norm_w': _L0_attn_b_in['o_norm_w'], 'L0_attn_b_Wo': _L0_attn_b_in['Wo'], 'L0_ffn_Wg': _L0_ffn_in['Wg'], 'L0_ffn_bg': _L0_ffn_in['bg'], 'L0_ffn_Wgate': _L0_ffn_in['Wgate'], 'L0_ffn_bgate': _L0_ffn_in['bgate'], 'L0_ffn_Wup': _L0_ffn_in['Wup'], 'L0_ffn_bup': _L0_ffn_in['bup'], 'L0_ffn_Wdown': _L0_ffn_in['Wdown'], 'L0_ffn_bdown': _L0_ffn_in['bdown'], 'L0_ffn_Ws_up': _L0_ffn_in['Ws_up'], 'L0_ffn_bs_up': _L0_ffn_in['bs_up'], 'L0_ffn_Ws_down': _L0_ffn_in['Ws_down'], 'L0_ffn_bs_down': _L0_ffn_in['bs_down']}
    _x0 = _d['L0_attn_a_x']
    _d['L0_attn_a_x'] = jax.random.normal(jax.random.fold_in(jax.random.key(seed), 1), (1, 2048, 512), dtype=_x0.dtype)
    del _x0
    return _d

def reference(L0_attn_a_x, L0_attn_a_Wq, L0_attn_a_Wk, L0_attn_a_Wv, L0_attn_a_Wo, L0_attn_b_Wq, L0_attn_b_Wk, L0_attn_b_Wv, L0_attn_b_conv_q_w, L0_attn_b_conv_q_b, L0_attn_b_conv_k_w, L0_attn_b_conv_k_b, L0_attn_b_conv_v_w, L0_attn_b_conv_v_b, L0_attn_b_Wfa, L0_attn_b_Wfb, L0_attn_b_A_log, L0_attn_b_dt_bias, L0_attn_b_Wb, L0_attn_b_Wga, L0_attn_b_Wgb, L0_attn_b_o_norm_w, L0_attn_b_Wo, L0_ffn_Wg, L0_ffn_bg, L0_ffn_Wgate, L0_ffn_bgate, L0_ffn_Wup, L0_ffn_bup, L0_ffn_Wdown, L0_ffn_bdown, L0_ffn_Ws_up, L0_ffn_bs_up, L0_ffn_Ws_down, L0_ffn_bs_down):

    def _L0_attn_a_ref(x, Wq, Wk, Wv, Wo):
        import jax, jax.numpy as jnp
        import numpy as np
        EMBED_DIM = 512
        NUM_HEADS = 32
        HEAD_DIM = EMBED_DIM // NUM_HEADS
        BATCH = 2
        SEQ_LEN = 512
        q = jnp.einsum('bse,ef->bsf', x, Wq)
        k = jnp.einsum('bse,ef->bsf', x, Wk)
        v = jnp.einsum('bse,ef->bsf', x, Wv)
        qT = jnp.swapaxes(q, 1, 2)
        kT = jnp.swapaxes(k, 1, 2)
        vT = jnp.swapaxes(v, 1, 2)
        attn_scores = jnp.einsum('bes,bfs->bef', qT, kT) / np.sqrt(HEAD_DIM)
        attn_weights = jax.nn.softmax(attn_scores, axis=-1)
        attn_output = jnp.einsum('bef,bfs->bes', attn_weights, vT)
        attn_output = jnp.swapaxes(attn_output, 1, 2)
        return jnp.einsum('bse,ef->bsf', attn_output, Wo)

    def _L0_attn_b_ref(x, Wq, Wk, Wv, conv_q_w, conv_q_b, conv_k_w, conv_k_b, conv_v_w, conv_v_b, Wfa, Wfb, A_log, dt_bias, Wb, Wga, Wgb, o_norm_w, Wo):
        import jax, jax.numpy as jnp
        import numpy as np
        from jax import lax
        B, T = (2, 512)
        HID = 512
        H, K, KC = (16, 128, 4)
        D = H * K
        EPS = 1e-05
        SCALE = K ** (-0.5)

        def causal_conv_silu(x, w, b):
            xp = jnp.pad(jnp.swapaxes(x, 1, 2), ((0, 0), (0, 0), (KC - 1, 0)))
            y = lax.conv_general_dilated(xp, w[:, None, :], (1,), 'VALID', feature_group_count=D)
            return jax.nn.silu(jnp.swapaxes(y, 1, 2) + b)

        def l2norm(x):
            return x * lax.rsqrt(jnp.sum(x * x, -1, keepdims=True) + 1e-06)

        def kda_scan(q, k, v, g, beta):
            qT, kT, vT, gT, bT = (jnp.moveaxis(a, 1, 0) for a in (q, k, v, g, beta))
            S0 = jnp.zeros((q.shape[0], H, K, K), q.dtype)

            def step(S, inp):
                qt, kt, vt, gt, bt = inp
                S = S * jnp.exp(gt)[..., None]
                vd = (vt - jnp.einsum('bhkv,bhk->bhv', S, kt)) * bt[..., None]
                S = S + kt[..., None] * vd[:, :, None, :]
                return (S, jnp.einsum('bhkv,bhk->bhv', S, qt))
            _, o = lax.scan(step, S0, (qT, kT, vT, gT, bT))
            return jnp.moveaxis(o, 0, 1)

        def _forward(x, Wq, Wk, Wv, conv_q_w, conv_q_b, conv_k_w, conv_k_b, conv_v_w, conv_v_b, Wfa, Wfb, A_log, dt_bias, Wb, Wga, Wgb, o_norm_w, Wo):
            b, t = x.shape[:2]
            q = causal_conv_silu(x @ Wq, conv_q_w, conv_q_b).reshape(b, t, H, K)
            k = causal_conv_silu(x @ Wk, conv_k_w, conv_k_b).reshape(b, t, H, K)
            v = causal_conv_silu(x @ Wv, conv_v_w, conv_v_b).reshape(b, t, H, K)
            g = jax.nn.softplus(x @ Wfa @ Wfb + dt_bias).reshape(b, t, H, K)
            g = -jnp.exp(A_log)[None, None, :, None] * g
            beta = jax.nn.sigmoid(x @ Wb)
            q = l2norm(q) * SCALE
            k = l2norm(k)
            o = kda_scan(q, k, v, g, beta)
            gate = (x @ Wga @ Wgb).reshape(b, t, H, K)
            var = jnp.mean(o * o, -1, keepdims=True)
            o = o * lax.rsqrt(var + EPS) * o_norm_w * jax.nn.sigmoid(gate)
            return o.reshape(b, t, D) @ Wo
        return _forward(x, Wq, Wk, Wv, conv_q_w, conv_q_b, conv_k_w, conv_k_b, conv_v_w, conv_v_b, Wfa, Wfb, A_log, dt_bias, Wb, Wga, Wgb, o_norm_w, Wo)

    def _L0_ffn_ref(x, Wg, bg, Wgate, bgate, Wup, bup, Wdown, bdown, Ws_up, bs_up, Ws_down, bs_down):
        import jax, jax.numpy as jnp
        import numpy as np
        B, S, D = (4, 512, 512)
        E = 8
        N_SHARE = 2
        N_ROUTED = E - N_SHARE
        H = 2048 // E
        b, s, d = x.shape
        T = b * s
        n = Wgate.shape[0]
        xf = x.reshape(T, d)
        gate = xf @ Wg + bg
        vals, ids = jax.lax.top_k(gate, n)
        rows = jnp.arange(T)[:, None]
        masked = jnp.full_like(gate, -jnp.inf).at[rows, ids].set(vals)
        probs = jax.nn.softmax(masked, axis=-1)
        routed_mask = (ids[:, :, None] == jnp.arange(n)).any(axis=1)
        w = probs[:, :n] * routed_mask
        g = jnp.einsum('td,ndh->tnh', xf, Wgate) + bgate
        u = jnp.einsum('td,ndh->tnh', xf, Wup) + bup
        h = jax.nn.silu(g) * u
        eo = jnp.einsum('tnh,nhd->tnd', h, Wdown) + bdown
        routed_out = jnp.einsum('tnd,tn->td', eo, w)
        share = jax.nn.silu(xf @ Ws_up + bs_up) @ Ws_down + bs_down
        return (routed_out + share).reshape(b, s, d)
    x = L0_attn_a_x
    x = x + _L0_attn_a_ref(_layernorm(x, axis=-1), L0_attn_a_Wq, L0_attn_a_Wk, L0_attn_a_Wv, L0_attn_a_Wo)
    x = x + _L0_ffn_ref(_layernorm(x, axis=-1), L0_ffn_Wg, L0_ffn_bg, L0_ffn_Wgate, L0_ffn_bgate, L0_ffn_Wup, L0_ffn_bup, L0_ffn_Wdown, L0_ffn_bdown, L0_ffn_Ws_up, L0_ffn_bs_up, L0_ffn_Ws_down, L0_ffn_bs_down)
    x = x + _L0_attn_b_ref(_layernorm(x, axis=-1), L0_attn_b_Wq, L0_attn_b_Wk, L0_attn_b_Wv, L0_attn_b_conv_q_w, L0_attn_b_conv_q_b, L0_attn_b_conv_k_w, L0_attn_b_conv_k_b, L0_attn_b_conv_v_w, L0_attn_b_conv_v_b, L0_attn_b_Wfa, L0_attn_b_Wfb, L0_attn_b_A_log, L0_attn_b_dt_bias, L0_attn_b_Wb, L0_attn_b_Wga, L0_attn_b_Wgb, L0_attn_b_o_norm_w, L0_attn_b_Wo)
    x = x + _L0_ffn_ref(_layernorm(x, axis=-1), L0_ffn_Wg, L0_ffn_bg, L0_ffn_Wgate, L0_ffn_bgate, L0_ffn_Wup, L0_ffn_bup, L0_ffn_Wdown, L0_ffn_bdown, L0_ffn_Ws_up, L0_ffn_bs_up, L0_ffn_Ws_down, L0_ffn_bs_down)
    return x

_drawn_inputs = setup_inputs


def setup_inputs(seed=0):
    import zlib

    import numpy as np

    out = dict(_drawn_inputs(seed))
    spreads = {'L0_attn_b_conv_q_b': (0.0, 0.375),
     'L0_attn_b_conv_k_b': (0.0, 0.366),
     'L0_attn_b_conv_v_b': (0.0, 0.367),
     'L0_attn_b_dt_bias': (0.0, 0.8),
     'L0_attn_b_o_norm_w': (1.0, 0.6),
     'L0_ffn_bg': (0.0, 0.8),
     'L0_ffn_bgate': (0.0, 0.8),
     'L0_ffn_bup': (0.0, 0.8),
     'L0_ffn_bdown': (0.0, 0.1),
     'L0_ffn_bs_up': (0.0, 0.1),
     'L0_ffn_bs_down': (0.0, 0.1)}
    factors = {'L0_attn_b_Wfa': 8.0,
     'L0_attn_b_Wfb': 8.0,
     'L0_attn_b_A_log': 8.0,
     'L0_attn_b_Wb': 6.166,
     'L0_attn_b_Wga': 8.0,
     'L0_attn_b_Wgb': 8.0,
     'L0_ffn_Wgate': 3.073,
     'L0_ffn_Wup': 3.01,
     'L0_ffn_Wdown': 2.945}
    for name, (base, spread) in spreads.items():
        noise = np.random.default_rng([zlib.crc32(name.encode()), seed]).standard_normal(out[name].shape)
        drawn = base * np.exp(spread * noise) if base else spread * noise
        out[name] = jnp.asarray(drawn.astype(out[name].dtype))
    for name, factor in factors.items():
        out[name] = (out[name] * factor).astype(out[name].dtype)
    return out
```

```python
from contextlib import ExitStack, contextmanager

import concourse.bass as bass
from concourse import mybir

F32 = mybir.dt.float32
I32 = mybir.dt.int32
ALU = mybir.AluOpType
ACT = mybir.ActivationFunctionType
AX = mybir.AxisListType

P = 128
T = 2048
D = 512
NT = T // P
KC = D // P
EPS = 1e-5

NR = 6
NE = 8
FH = 256
HC = FH // P
SC = D // P
FT = 512
FN = T // FT

H = 16
HG = 4
HJ = 4
C = 32
TT = 256
TN = T // TT
NC_ = TT // C
NG = HG * NC_
LEVELS = 5
KEPS = 1e-6
UNITS = 2 * (LEVELS + 1)
DVE_PER_STEP = 241

K_ID, K_ONE, K_JM, K_MASK, K_EPS5, K_EPS6, K_JLT = 0, 128, 256, 260, 452, 453, 454
K_N = 518


def constants():
    import numpy as np
    c = np.zeros((P, K_N), np.float32)
    p = np.arange(P)
    c[:, K_ID:K_ID + P] = np.eye(P)
    c[:, K_ONE:K_ONE + P] = 1.0
    c[p, K_JM + p // C] = 1.0
    s = p % C
    for t in range(C):
        c[s == t, K_MASK + t] = 1.0
    for lv in range(1, LEVELS + 1):
        m = 1 << (lv - 1)
        for n in range(C // 2):
            seg, k = n // m, n % m
            ok = (s // (2 * m) == seg) & (s % (2 * m) < m)
            c[ok, K_MASK + 32 * lv + n] = 1.0
    c[:, K_EPS5] = EPS
    c[:, K_EPS6] = KEPS
    for i in range(NE):
        for j in range(i):
            c[:, K_JLT + i * NE + j] = 1.0
    return c


class Order:

    def __init__(self, eng, sem, base=0):
        self.eng, self.sem, self.base, self.n = eng, sem, base, 0

    def done(self, ins):
        ins.then_inc(self.sem, 1)
        self.n += 1
        return self.n

    def wait(self, n=None):
        self.eng.wait_ge(self.sem, self.base + (self.n if n is None else n))


@contextmanager
def stage_semaphores(nc):
    used = []

    def sem(name):
        used.append(nc.alloc_semaphore(name=name))
        return used[-1]
    yield sem
    nc.clear_and_free_semaphores(used)
    nc.all_engine_barrier()


def norm_stage(nc, tag, x_sb, xnt, ps, cst, gram=False):
    with ExitStack() as c2:
        sem = c2.enter_context(stage_semaphores(nc))
        sb = lambda n, s: c2.enter_context(nc.sbuf_tensor(tag + n, s, F32))
        st = sb("stats", [P, NT, 6])
        mv = sb("meanvar", [P, NT, 2])
        rstd = sb("rstd", [P, NT])
        shift = sb("shift", [P, NT])
        xn = sb("xn", [P, 2, D])
        order = sem(tag + "dve_order")
        var_ready = sem(tag + "var_ready")
        std_ready = sem(tag + "std_ready")
        xn_ready = [sem(tag + f"xn_ready{b}") for b in range(2)]
        xn_read = [sem(tag + f"xn_read{b}") for b in range(2)]
        bank_free = [sem(tag + f"bank_free{b}") for b in range(2)]
        with nc.Block() as block:

            @block.vector
            def _(dve):
                o = Order(dve, order)
                for i in range(NT):
                    o.done(dve.bn_stats(st[:, i, :], x_sb[:, i, :]))
                o.wait()
                for i in range(NT):
                    last = dve.bn_aggr(mv[:, i, :], st[:, i, :])
                last.then_inc(var_ready, 1)
                dve.wait_ge(std_ready, 1)
                o.done(dve.reciprocal(rstd[:, :], rstd[:, :]))
                o.wait()
                o.done(dve.scalar_tensor_tensor(shift[:, :], mv[:, :, 0], -1.0, rstd[:, :], ALU.mult, ALU.mult))
                o.wait()
                with dve.Fori(0, NT // 2, 1) as ii:
                    for b in range(2):
                        i = ii * 2 + b
                        dve.wait_ge(xn_read[b], ii)
                        dve.tensor_scalar(xn[:, b, :], x_sb[:, i, :], rstd[:, bass.ds(i, 1)], shift[:, bass.ds(i, 1)],
                                          ALU.mult, ALU.add).then_inc(xn_ready[b], 1)

            @block.scalar
            def _(act):
                act.wait_ge(var_ready, 1)
                act.activation(rstd[:, :], mv[:, :, 1], ACT.Sqrt, bias=cst[:, K_EPS5:K_EPS5 + 1]).then_inc(std_ready, 1)
                with act.Fori(0, NT // 2, 1) as ii:
                    for b in range(2):
                        i = ii * 2 + b
                        act.wait_ge(xn_read[b], ii + 1)
                        act.activation(xnt[:, :, bass.ds(i * P, P)],
                                       ps[:, b, :].rearrange("p (k t) -> p k t", k=KC), ACT.Copy).then_inc(bank_free[b], 1)

            @block.tensor
            def _(pe):
                def tile(ii, first):
                    for b in range(2):
                        pe.wait_ge(xn_ready[b], ii + 1)
                        if gram:
                            for e in range(KC):
                                pe.matmul(ps[:, 4 + e, :], xn[:, b, e * P:(e + 1) * P], xn[:, b, :],
                                          start=(first and b == 0), stop=True, skip_group_check=True)
                        pe.wait_ge(bank_free[b], ii)
                        for k in range(KC):
                            last = pe.transpose(ps[:, b, k * P:(k + 1) * P], xn[:, b, k * P:(k + 1) * P],
                                                cst[:, K_ID:K_ID + P])
                        last.then_inc(xn_read[b], 1)
                tile(0, True)
                with pe.Fori(1, NT // 2, 1) as ii:
                    tile(ii, False)


def attention_stage(nc, x_sb, xnt, ps, cst, dram):
    with ExitStack() as c2:
        sem = c2.enter_context(stage_semaphores(nc))
        sb = lambda n, s: c2.enter_context(nc.sbuf_tensor("at_" + n, s, F32))
        w = {n: sb(n, [P, KC, D]) for n in ("wq", "wk", "wo", "wvt")}
        g, t1, pr, r1, m = (sb(n, [P, KC, D]) for n in ("g", "t1", "pr", "r1", "m"))
        mx, nmx, rs, rc = (sb(n, [P, KC]) for n in ("mx", "nmx", "rs", "rc"))
        w_in = {n: sem("at_in_" + n) for n in w}
        g_ready, t1_ps, t1_ready, s_ps, neg_max, exp_ready, p_ready, r1_ps, r1_ready, m_ps, m_ready, order = (
            sem("at_" + n) for n in ("g_ready", "t1_ps", "t1_ready", "s_ps", "neg_max", "exp_ready", "p_ready",
                                     "r1_ps", "r1_ready", "m_ps", "m_ready", "order"))
        y_ps = [sem(f"at_y_ps{b}") for b in range(4)]
        y_read = [sem(f"at_y_read{b}") for b in range(4)]
        with nc.Block() as block:

            @block.sync
            def _(sp):
                for n in ("wk", "wq", "wo", "wvt"):
                    sp.dma_start(w[n][:, :, :], dram[n].rearrange("(k p) n -> p k n", p=P)).then_inc(w_in[n], 16)

            @block.tensor
            def _(pe):
                def product(banks, lhs, rhs, signal):
                    for e in range(KC):
                        for k in range(KC):
                            last = pe.matmul(ps[:, banks + e, :], lhs[:, k, e * P:(e + 1) * P], rhs[:, k, :],
                                             start=(k == 0), stop=(k == KC - 1))
                        last.then_inc(signal, 1)
                pe.wait_ge(w_in["wk"], 16)
                pe.wait_ge(g_ready, KC)
                product(0, g, w["wk"], t1_ps)
                pe.wait_ge(w_in["wq"], 16)
                pe.wait_ge(t1_ready, KC)
                product(4, w["wq"], t1, s_ps)
                pe.wait_ge(w_in["wo"], 16)
                pe.wait_ge(p_ready, KC)
                product(0, pr, w["wo"], r1_ps)
                pe.wait_ge(w_in["wvt"], 16)
                pe.wait_ge(r1_ready, KC)
                product(4, w["wvt"], r1, m_ps)
                pe.wait_ge(m_ready, KC)
                for i in range(NT):
                    b = i % 4
                    if i >= 4:
                        pe.wait_ge(y_read[b], i // 4)
                    for k in range(KC):
                        last = pe.matmul(ps[:, b, :], xnt[:, k, i * P:(i + 1) * P], m[:, k, :],
                                         start=(k == 0), stop=(k == KC - 1))
                    last.then_inc(y_ps[b], 1)

            @block.scalar
            def _(act):
                for e in range(KC):
                    act.activation(g[:, e, :], ps[:, 4 + e, :], ACT.Copy).then_inc(g_ready, 1)
                for e in range(KC):
                    act.wait_ge(t1_ps, e + 1)
                    act.activation(t1[:, e, :], ps[:, e, :], ACT.Copy).then_inc(t1_ready, 1)
                for e in range(KC):
                    act.wait_ge(neg_max, e + 1)
                    act.activation(pr[:, e, :], ps[:, 4 + e, :], ACT.Exp, bias=nmx[:, e:e + 1], scale=0.25,
                                   accum_out=rs[:, e:e + 1]).then_inc(exp_ready, 1)
                for e in range(KC):
                    act.wait_ge(r1_ps, e + 1)
                    act.activation(r1[:, e, :], ps[:, e, :], ACT.Copy).then_inc(r1_ready, 1)
                for e in range(KC):
                    act.wait_ge(m_ps, e + 1)
                    act.activation(m[:, e, :], ps[:, 4 + e, :], ACT.Copy).then_inc(m_ready, 1)

            @block.vector
            def _(dve):
                o = Order(dve, order)
                for e in range(KC):
                    dve.wait_ge(s_ps, e + 1)
                    o.done(dve.reduce_max(mx[:, e:e + 1], ps[:, 4 + e, :], AX.X))
                    o.wait()
                    dve.tensor_scalar(nmx[:, e:e + 1], mx[:, e:e + 1], -0.25, None, ALU.mult).then_inc(neg_max, 1)
                for e in range(KC):
                    dve.wait_ge(exp_ready, e + 1)
                    o.done(dve.reciprocal(rc[:, e:e + 1], rs[:, e:e + 1]))
                    o.wait()
                    dve.tensor_scalar(pr[:, e, :], pr[:, e, :], rc[:, e:e + 1], None, ALU.mult).then_inc(p_ready, 1)
                for i in range(NT):
                    b = i % 4
                    dve.wait_ge(y_ps[b], i // 4 + 1)
                    dve.tensor_tensor(x_sb[:, i, :], ps[:, b, :], x_sb[:, i, :], ALU.add).then_inc(y_read[b], 1)


def ffn_stage(nc, tag, x_sb, xnt, ps, cst, dram, store_to):
    with ExitStack() as c2:
        sem = c2.enter_context(stage_semaphores(nc))
        sb = lambda n, s: c2.enter_context(nc.sbuf_tensor(tag + n, s, F32))
        wg = sb("wgate", [P, NR, KC, FH])
        wu = sb("wup", [P, NR, KC, FH])
        wd = sb("wdown", [P, NR, HC, D])
        wsu = sb("wsup", [P, KC, D])
        wsd = sb("wsdown", [P, SC, D])
        wr = sb("wrouter", [P, KC, NE])
        br = sb("brouter", [P, NE])
        bg = sb("bgate", [P, NR * HC])
        bu = sb("bup", [P, NR * HC])
        bs = sb("bshared", [P, SC])
        bd = sb("bdown", [NR + 1, D])
        sel = sb("select", [NE, NR, P])
        wt = sb("weights_t", [NE, T])
        wts = sb("weights_t_step", [NE, FT])
        wb = sb("weights_b", [P, NR, FT])
        act_g = sb("act_g", [P, 2, FT])
        hid = sb("hidden", [P, 2, FT])
        lg = sb("logits", [P, NT, NE])
        pw = sb("probs", [P, NT, NE])
        mxl = sb("max", [P, NT])
        sm = sb("sum", [P, NT])
        cmp_a = act_g[:, :, :].rearrange("p a (b c d) -> p (a b) c d", c=NE, d=NE)
        cmp_b = hid[:, :, :].rearrange("p a (b c d) -> p (a b) c d", c=NE, d=NE)
        names = ("w_in", "wr_in", "wsh_in", "order", "logits_ps", "logits_max", "exp_ready", "probs_ready", "wt_ps",
                 "wt_ready", "acc_ps", "acc_read", "stored", "wts_ready", "bcast_ps", "bcast_ready", "step_read")
        (w_in, wr_in, wsh_in, order, logits_ps, logits_max, exp_ready, probs_ready, wt_ps, wt_ready, acc_ps,
         acc_read, stored, wts_ready, bcast_ps, bcast_ready, step_read) = (sem(tag + n) for n in names)
        up_ps, gate_ready, hid_ready, hid_read = ([sem(tag + f"{n}{b}") for b in range(2)]
                                                  for n in ("up_ps", "gate_ready", "hid_ready", "hid_read"))
        units = [(n, c) for n in range(NR) for c in range(HC)] + [(NR, c) for c in range(SC)]
        NU = len(units)
        per_slot = NU // 2
        x_dram = store_to.rearrange("(n p) d -> n p d", p=P)
        with nc.Block() as block:

            @block.sync
            def _(sp):
                sp.dma_start(wr[:, :, :], dram["router"]).then_inc(wr_in, 16)
                sp.dma_start(br[:, :], dram["brouter"]).then_inc(wr_in, 16)
                for dst, name in ((wg, "wgate"), (wu, "wup"), (wd, "wdown"), (wsu, "wsup"), (wsd, "wsdown")):
                    sp.dma_start(dst[:], dram[name]).then_inc(w_in, 16)
                for dst, name in ((bg, "bgate"), (bu, "bup"), (bs, "bsup"), (bd, "bdown"), (sel, "select")):
                    sp.dma_start(dst[:], dram[name]).then_inc(w_in, 16)
                with sp.Fori(0, FN, 1) as s:
                    sp.wait_ge(acc_read, s * 4 + 4)
                    for i in range(4):
                        sp.dma_start(x_dram[s * 4 + i], x_sb[:, s * 4 + i, :]).then_inc(stored, 16)
                sp.wait_ge(stored, 16 * NT)

            @block.tensor
            def _(pe):
                pe.wait_ge(wr_in, 32)
                for i in range(NT):
                    for k in range(KC):
                        last = pe.matmul(ps[:, 0, i * NE:(i + 1) * NE], xnt[:, k, i * P:(i + 1) * P], wr[:, k, :],
                                         start=(k == 0), stop=(k == KC - 1))
                last.then_inc(logits_ps, 1)
                pe.wait_ge(probs_ready, 1)
                for i in range(NT):
                    last = pe.transpose(ps[0:NE, 4 + i // 4, (i % 4) * P:(i % 4 + 1) * P], pw[:, i, :],
                                        cst[:, K_ID:K_ID + P])
                last.then_inc(wt_ps, 1)
                pe.wait_ge(w_in, 16 * 10)
                with pe.Fori(0, FN, 1) as s:
                    pe.wait_ge(wts_ready, s + 1)
                    for n in range(NR):
                        if n >= 4:
                            pe.wait_ge(bcast_ready, s * NR + n - 3)
                        if n == 0:
                            pe.wait_ge(hid_ready[0], s * per_slot)
                            pe.wait_ge(hid_ready[1], s * per_slot)
                        last = pe.matmul(ps[:, n % 4, :], sel[:, n, :], wts[:, :],
                                         start=True, stop=True)
                        last.then_inc(bcast_ps, 1)
                    pe.wait_ge(bcast_ready, s * NR + NR)

                    def up(u):
                        n, c = units[u]
                        b = u % 2
                        pe.wait_ge(hid_ready[b], s * per_slot + u // 2)
                        for k in range(KC):
                            lhs = wg[:, n, k, c * P:(c + 1) * P] if n < NR else wsu[:, k, c * P:(c + 1) * P]
                            last = pe.matmul(ps[:, 2 * b, :], lhs, xnt[:, k, bass.ds(s * FT, FT)],
                                             start=(k == 0), stop=(k == KC - 1))
                        if n < NR:
                            for k in range(KC):
                                last = pe.matmul(ps[:, 2 * b + 1, :], wu[:, n, k, c * P:(c + 1) * P],
                                                 xnt[:, k, bass.ds(s * FT, FT)], start=(k == 0), stop=(k == KC - 1))
                        last.then_inc(up_ps[b], 1)

                    def down(u):
                        n, c = units[u]
                        b = u % 2
                        pe.wait_ge(hid_ready[b], s * per_slot + (u // 2 + 1))
                        if u == 0:
                            pe.wait_ge(acc_read, s * 4)
                        for i in range(4):
                            rhs = wd[:, n, c, :] if n < NR else wsd[:, c, :]
                            last = pe.matmul(ps[:, 4 + i, :], hid[:, b, i * P:(i + 1) * P], rhs,
                                             start=(u == 0), stop=False)
                        last.then_inc(hid_read[b], 1)

                    up(0)
                    for u in range(1, NU):
                        up(u)
                        down(u - 1)
                    down(NU - 1)
                    for i in range(4):
                        last = pe.matmul(ps[:, 4 + i, :], wts[0:NR + 1, i * P:(i + 1) * P], bd[:, :],
                                         start=False, stop=True)
                    last.then_inc(acc_ps, 1)

            @block.scalar
            def _(act):
                act.wait_ge(logits_max, 1)
                act.activation(pw[:, :, :], lg[:, :, :], ACT.Exp).then_inc(exp_ready, 1)
                with act.Fori(0, FN, 1) as s:
                    for n in range(NR):
                        act.wait_ge(bcast_ps, s * NR + n + 1)
                        act.activation(wb[:, n, :], ps[:, n % 4, :], ACT.Copy).then_inc(bcast_ready, 1)
                    for u in range(NU):
                        n, c = units[u]
                        b = u % 2
                        act.wait_ge(up_ps[b], s * per_slot + (u // 2 + 1))
                        if n < NR:
                            act.wait_ge(hid_ready[b], s * per_slot + u // 2)
                            act.activation(act_g[:, b, :], ps[:, 2 * b, :], ACT.Silu,
                                           bias=bg[:, n * HC + c:n * HC + c + 1]).then_inc(gate_ready[b], 1)
                        else:
                            act.wait_ge(hid_read[b], s * per_slot + u // 2)
                            act.activation(hid[:, b, :], ps[:, 2 * b, :], ACT.Silu,
                                           bias=bs[:, c:c + 1]).then_inc(hid_ready[b], 1)

            @block.vector
            def _(dve):
                o = Order(dve, order)
                step = lambda ins: (o.done(ins), o.wait())
                dve.wait_ge(wr_in, 32)
                dve.wait_ge(logits_ps, 1)
                lgp = ps[:, 0, 0:NT * NE].rearrange("p (i e) -> p i e", e=NE)
                step(dve.tensor_tensor(lg[:, :, :], lgp, br[:, :].unsqueeze(1).broadcast_to([P, NT, NE]), ALU.add))
                step(dve.tensor_reduce(mxl[:, :], lg[:, :, :], AX.X, ALU.max))
                row = lg[:, :, :].unsqueeze(3).broadcast_to([P, NT, NE, NE])
                col = lg[:, :, :].unsqueeze(2).broadcast_to([P, NT, NE, NE])
                earlier = cst[:, K_JLT:K_JLT + NE * NE].rearrange("p (c d) -> p c d", c=NE).unsqueeze(1)
                dve.tensor_tensor(cmp_a, col, row, ALU.is_gt)
                step(dve.tensor_tensor(cmp_b, col, row, ALU.is_equal))
                step(dve.tensor_tensor(cmp_b, cmp_b, earlier.broadcast_to([P, NT, NE, NE]), ALU.mult))
                step(dve.tensor_tensor(cmp_a, cmp_a, cmp_b, ALU.add))
                ahead = hid[:, 0, 0:NT * NE].rearrange("p (i e) -> p i e", e=NE)
                step(dve.tensor_reduce(ahead, cmp_a, AX.X, ALU.add))
                step(dve.tensor_scalar(ahead, ahead, float(NR) - 0.5, None, ALU.is_lt))
                dve.tensor_tensor(lg[:, :, :], lg[:, :, :], mxl[:, :].unsqueeze(2).broadcast_to([P, NT, NE]),
                                  ALU.subtract).then_inc(logits_max, 1)
                dve.wait_ge(exp_ready, 1)
                step(dve.tensor_tensor(pw[:, :, :], pw[:, :, :], ahead, ALU.mult))
                step(dve.tensor_reduce(sm[:, :], pw[:, :, :], AX.X, ALU.add))
                step(dve.reciprocal(sm[:, :], sm[:, :]))
                step(dve.tensor_tensor(pw[:, :, :], pw[:, :, :], sm[:, :].unsqueeze(2).broadcast_to([P, NT, NE]),
                                       ALU.mult))
                dve.memset(pw[:, :, NR:NR + 1], 1.0).then_inc(probs_ready, 1)
                dve.wait_ge(wt_ps, 1)
                for q in range(4):
                    last = dve.tensor_copy(wt[:, q * FT:(q + 1) * FT], ps[0:NE, 4 + q, :])
                last.then_inc(wt_ready, 1)
                dve.wait_ge(wt_ready, 1)
                dve.wait_ge(w_in, 16 * 10)
                with dve.Fori(0, FN, 1) as s:
                    dve.wait_ge(acc_ps, s)
                    dve.tensor_copy(wts[:, :], wt[:, bass.ds(s * FT, FT)]).then_inc(wts_ready, 1)
                    dve.wait_ge(bcast_ready, s * NR + NR)
                    for u in range(NR * HC):
                        n, c = units[u]
                        b = u % 2
                        dve.wait_ge(up_ps[b], s * per_slot + (u // 2 + 1))
                        dve.wait_ge(gate_ready[b], s * NR + (u // 2 + 1))
                        dve.scalar_tensor_tensor(act_g[:, b, :], ps[:, 2 * b + 1, :], bu[:, n * HC + c:n * HC + c + 1],
                                                 act_g[:, b, :], ALU.add, ALU.mult).then_inc(step_read, 1)
                        dve.wait_ge(step_read, s * NR * HC + (u + 1))
                        dve.wait_ge(hid_read[b], s * per_slot + u // 2)
                        dve.tensor_tensor(hid[:, b, :], act_g[:, b, :], wb[:, n, :], ALU.mult).then_inc(hid_ready[b], 1)
                    dve.wait_ge(acc_ps, s + 1)
                    for i in range(4):
                        dve.tensor_tensor(x_sb[:, s * 4 + i, :], ps[:, 4 + i, :], x_sb[:, s * 4 + i, :],
                                          ALU.add).then_inc(acc_read, 1)


def delta_stage(nc, x_in, x_out, xnt_dram, ps, cst, d):
    with ExitStack() as c2:
        sem = c2.enter_context(stage_semaphores(nc))
        sb = lambda n, s: c2.enter_context(nc.sbuf_tensor("dl_" + n, s, F32))
        xt = sb("xt", [P, KC, TT])
        state = sb("state", [P, H, P])
        wab = sb("wab", [P, KC, 2 * P + H])
        wfb = sb("wfb", [P, H * P])
        wgb = sb("wgb", [P, H * P])
        wqkv = sb("wqkv", [P, 2, 3, KC, P])
        par = sb("par", [P, H, 17])
        nega = sb("nega", [P, H])
        onw = sb("onw", [P, 1])
        kq = sb("kq", [P, 2, NG, HJ, C])
        kk = sb("kk", [P, NG, HJ, C])
        dec = sb("dec", [P, NG, HJ, C])
        val = sb("val", [P, NG, P])
        amat = sb("amat", [P, NG, 2, C])
        bdt = sb("bdt", [P, NG, HJ, C])
        bda = sb("bda", [P, NG, HJ, C])
        halo = sb("halo", [P, H, 3, 3])
        tot = sb("tot", [P, NG, HJ])
        kap = sb("kap", [P, 2 * NG])
        nkap = sb("nkap", [P, NG])
        oss = sb("oss", [P, NG])
        ofac = sb("ofac", [P, NG])
        fg = sb("fg", [P, 2, TT])
        beta = sb("beta", [H, TT])
        kapt = sb("kapt", [NG, P])
        kb = sb("kb", [P, C])
        bb = sb("bb", [P, C])
        rbuf = sb("rbuf", [P, 2, P])
        ubuf = sb("ubuf", [P, 2, P])
        junk = sb("junk", [P, 2, P])
        waited = sb("waited", [P, UNITS + HG])
        tmp = sb("tmp", [P, 7200])
        raw = [tmp[:, b * 778:b * 778 + 777].rearrange("p (a t) -> p a t", a=3) for b in range(2)]
        cv = [tmp[:, 1556 + b * 768:1556 + (b + 1) * 768].rearrange("p (a t) -> p a t", a=3) for b in range(2)]
        vt = tmp[:, 3092:4116].rearrange("p (c j t) -> p c j t", j=HJ, t=C)
        sq = tmp[:, 4116:6164].rearrange("p (w c j t) -> p w c j t", w=2, j=HJ, t=C)
        sp_w = [tmp[:, n:n + 1024] for n in (0, 1024, 2048, 6164)]
        sp_ln = [tmp[:, n:n + 1024] for n in (4116, 5140)]
        sp_poly = tmp[:, 3092:4116]
        nm, zm, zt = (tmp[:, n * 1024:(n + 1) * 1024].rearrange("p (s t) -> p s t", s=C) for n in range(3))
        ubd = tmp[:, 0:1024].rearrange("p (b j v) -> p b j v", b=2, j=HJ)
        xio = tmp[:, 3072:4096].rearrange("p (n d) -> p n d", n=2)
        wo = [tmp[:, 4116 + n * 1024:4116 + (n + 1) * 1024].rearrange("p (h n) -> p h n", h=2) for n in range(2)]
        sg = [tmp[:, 6164 + n * TT:6164 + (n + 1) * TT] for n in range(2)]
        kkt = dec[:].rearrange("p g j t -> p g (j t)")
        ot = kk[:].rearrange("p g j t -> p (g j t)").rearrange("p (h t) -> p h t", h=H)
        by_head = lambda ap, h: ap[:, h // HJ * NC_:(h // HJ + 1) * NC_, h % HJ, :]
        by_group = lambda ap, hg: ap[:, hg * NC_:(hg + 1) * NC_].rearrange("p c j t -> p (c j t)")
        chunks = lambda ap: ap.rearrange("p (c t) -> p c t", t=C)

        a_dram = nc.dram_tensor("akk_blocks", [HG, NC_, HJ, C, C], F32).ap()
        t_dram = nc.dram_tensor("t_blocks", [HG, NC_, HJ, C, C], F32).ap()
        k_dram = nc.dram_tensor("inverse_norms", [NG, P], F32).ap()
        b_dram = nc.dram_tensor("betas", [HG, NC_, HJ, C], F32).ap()
        ident = cst[:, K_ID:K_ID + P]

        names = """setup const_ready xt_in fg_ps fg_ready beta_ps beta_ready beta_out beta_in halo_in halo_out proj_ps
            proj_read conv_done silu_done squared v_ps v_read v_rows sums_ps roots_ready kap_ready kapt_ps kapt_ready kapt_out
            kapt_in sp_log sp_sum decay_ready lvl_ps lvl_done a_out a_in t_ready t_out t_in bda_ready kkt_ps
            kkt_read tot_ready kps r_ready u_ps u_ready ubd_ready o_ps o_read s_ps s_read oss_ready ofac_var ofac_std
            o_scaled gate_ps gate_ready ot_ps ot_ready y_ps y_ready x_loaded x_stored unit_in dve_order act_order
            pool_order""".split()
        s = {n: sem("dl_" + n) for n in names}
        w_in = [sem(f"dl_w_in{b}") for b in range(2)]
        wo_in = [sem(f"dl_wo_in{b}") for b in range(2)]

        with nc.Block() as block:

            @block.sync
            def _(sp):
                for dst, src in ((wab, "dwa"), (wfb, "dwfb"), (wgb, "dwgb"), (par, "dheads"), (onw, "donorm")):
                    sp.dma_start(dst[:], d[src]).then_inc(s["setup"], 16)
                with sp.Fori(0, TN, 1) as i:
                    sp.wait_ge(s["proj_ps"], i * H)
                    sp.wait_ge(s["beta_ps"], i)
                    sp.dma_start(xt[:, :, :], xnt_dram[i]).then_inc(s["xt_in"], 16)
                    for h in range(H):
                        if h >= 2:
                            sp.wait_ge(s["proj_ps"], i * H + (h - 1))
                        sp.dma_start(wqkv[:, h % 2], d["dw_qkv"][h].rearrange("p a k n -> p a k n")
                                     ).then_inc(w_in[h % 2], 16)
                    sp.wait_ge(s["beta_ready"], i + 1)
                    sp.wait_ge(s["t_ready"], i)
                    for hg in range(HG):
                        sp.dma_start(b_dram[hg].rearrange("c j t -> j c t"),
                                     beta[HJ * hg:HJ * hg + HJ, :].rearrange("j (c t) -> j c t", t=C)
                                     ).then_inc(s["beta_out"], 16)
                    sp.wait_ge(s["beta_out"], (i + 1) * 16 * HG)
                    sp.dma_start(bb[:, :], b_dram.rearrange("g c j t -> (g c j) t")).then_inc(s["beta_in"], 16)
                    sp.wait_ge(s["kapt_ready"], i + 1)
                    sp.dma_start(k_dram, kapt[:, :]).then_inc(s["kapt_out"], 16)
                    sp.wait_ge(s["kapt_out"], (i + 1) * 16)
                    sp.dma_start(kb[:, :], k_dram.rearrange("g (j t) -> (g j) t", t=C)).then_inc(s["kapt_in"], 16)
                    sp.wait_ge(s["x_stored"], i * 32)
                    for n in range(2):
                        sp.dma_start(xio[:, n, :], x_in[bass.ds(i * TT + n * P, P), :]).then_inc(s["x_loaded"], 16)
                    sp.wait_ge(s["lvl_done"], (i + 1) * UNITS)
                    for j in range(HJ):
                        sp.dma_start(a_dram.rearrange("g c j s t -> j s (g c) t")[j],
                                     amat[C * j:C * j + C, :, 0, :]).then_inc(s["a_out"], 16)
                    sp.dma_start(zm, d["unit"]).then_inc(s["unit_in"], 16)
                    sp.wait_ge(s["a_out"], (i + 1) * 16 * HJ)
                    sp.dma_start(nm, a_dram.rearrange("g c j s t -> (g c j) s t")).then_inc(s["a_in"], 16)
                    sp.wait_ge(s["t_ready"], i + 1)
                    sp.dma_start(t_dram.rearrange("g c j s t -> (g c j) s t"), zm).then_inc(s["t_out"], 16)
                    sp.wait_ge(s["t_out"], (i + 1) * 16)
                    for j in range(HJ):
                        sp.dma_start(bdt[C * j:C * j + C, :, j, :],
                                     t_dram.rearrange("g c j s t -> j s (g c) t")[j]).then_inc(s["t_in"], 16)
                    for n in range(H // 2):
                        if n >= 2:
                            sp.wait_ge(s["y_ps"], i * (H // 2) + (n - 1))
                        sp.dma_start(wo[n % 2], d["dwo"][n]).then_inc(wo_in[n % 2], 16)
                    sp.wait_ge(s["y_ready"], i * 2 + 2)
                    for n in range(2):
                        sp.dma_start(x_out[bass.ds(i * TT + n * P, P), :], xio[:, n, :]).then_inc(s["x_stored"], 16)
                sp.wait_ge(s["x_stored"], TN * 32)

            def square(pool, i, h):
                j = h % HJ
                pool.wait_ge(s["silu_done"], i * H + (h + 1))
                if j == 0:
                    pool.wait_ge(s["sums_ps"], i * HG + h // HJ)
                k_, q_ = by_head(kk, h), by_head(kq[:, 1], h)
                pool.tensor_tensor(sq[:, 0, :, j, :], k_, k_, ALU.mult)
                pool.tensor_tensor(sq[:, 1, :, j, :], q_, q_, ALU.mult).then_inc(s["squared"], 1)

            @block.gpsimd
            def _(pool):
                o = Order(pool, s["pool_order"])
                o.done(pool.memset(halo[:], 0.0))
                o.done(pool.memset(bdt[:], 0.0))
                o.done(pool.memset(bda[:], 0.0))
                pool.memset(amat[:], 0.0).then_inc(s["const_ready"], 1)
                o.wait()
                with pool.Fori(0, TN, 1) as i:
                    pool.wait_ge(s["y_ready"], i * 2)

                    ones = cst[:, K_ONE:K_ONE + 1].unsqueeze(2).broadcast_to([P, 3, 3])

                    def halo_in(h):
                        pool.wait_ge(s["conv_done"], i * H + max(h - 1, 0))
                        pool.wait_ge(s["halo_out"], i * H + max(h - 1, 0))
                        pool.tensor_tensor(raw[h % 2][:, :, 0:3], halo[:, h], ones, ALU.mult).then_inc(s["halo_in"], 1)

                    halo_in(0)
                    for h in range(H):
                        if h + 1 < H:
                            halo_in(h + 1)
                        pool.wait_ge(s["proj_read"], i * H + (h + 1))
                        pool.wait_ge(s["halo_in"], i * H + (h + 1))
                        tail = raw[h % 2][:, :, TT:TT + 3]
                        pool.tensor_tensor(halo[:, h], tail, ones, ALU.mult).then_inc(s["halo_out"], 1)
                        if h >= 1:
                            square(pool, i, h - 1)
                    square(pool, i, H - 1)
                    pool.wait_ge(s["lvl_done"], (i + 1) * UNITS)
                    pool.wait_ge(s["kap_ready"], i + 1)
                    for j in range(HJ):
                        q = slice(C * j, C * j + C)
                        pool.tensor_tensor(bda[q, :, j, :], amat[q, :, 1, :],
                                           kap[q, 0:NG].unsqueeze(2).broadcast_to([C, NG, C]),
                                           ALU.mult).then_inc(s["bda_ready"], 1)

            @block.scalar
            def _(act):
                o = Order(act, s["act_order"])
                act.wait_ge(s["setup"], 80)
                o.done(act.activation(nega[:, :], par[:, :, 16], ACT.Exp))
                o.wait()
                act.activation(nega[:, :], nega[:, :], ACT.Copy, scale=-1.0).then_inc(s["act_order"], 1)
                act.wait_ge(s["act_order"], 2)
                with act.Fori(0, TN, 1) as i:
                    act.wait_ge(s["y_ready"], i * 2)
                    act.wait_ge(s["x_stored"], i * 32)
                    act.wait_ge(s["fg_ps"], (i + 1) * 2)
                    act.activation(fg[:, :, :], ps[:, 4, :].rearrange("p (a t) -> p a t", a=2),
                                   ACT.Copy).then_inc(s["fg_ready"], 1)

                    def silu(h):
                        j = h % HJ
                        act.wait_ge(s["conv_done"], i * H + (h + 1))
                        if j == 0:
                            act.wait_ge(s["v_ps"], i * HG + h // HJ)
                        act.activation(by_head(kq[:, 1], h), chunks(cv[h % 2][:, 0]), ACT.Silu)
                        act.activation(by_head(kk, h), chunks(cv[h % 2][:, 1]), ACT.Silu)
                        act.activation(vt[:, :, j, :], chunks(cv[h % 2][:, 2]), ACT.Silu).then_inc(s["silu_done"], 1)

                    def v_rows(hg):
                        act.wait_ge(s["v_ps"], i * HG + (hg + 1))
                        for n in range(2):
                            g0 = hg * NC_ + n * 4
                            last = act.activation(val[:, g0:g0 + 4, :], ps[:, 4 + n, :].rearrange("p (c v) -> p c v", c=4),
                                                  ACT.Copy)
                        last.then_inc(s["v_rows"], 1)

                    for h in range(H):
                        b = h % 2
                        act.wait_ge(s["proj_ps"], i * H + (h + 1))
                        act.wait_ge(s["conv_done"], i * H + max(h - 1, 0))
                        act.wait_ge(s["halo_out"], i * H + max(h - 1, 0))
                        act.wait_ge(s["silu_done"], i * H + max(h - 1, 0))
                        act.activation(raw[b][:, 0:2, 3:3 + TT], ps[:, 2 * b, :].rearrange("p (a t) -> p a t", a=2), ACT.Copy)
                        act.activation(raw[b][:, 2, 3:3 + TT], ps[:, 2 * b + 1, 0:TT], ACT.Copy)
                        for a in range(3):
                            act.activation(cv[b][:, a], ps[:, 2 * b + a // 2, (a % 2) * TT:(a % 2 + 1) * TT], ACT.Identity,
                                           bias=par[:, h, 12 + a:13 + a], scale=par[:, h, 4 * a + 3:4 * a + 4])
                        act.activation(by_head(dec, h), chunks(ps[:, 2 * b + 1, TT:2 * TT]), ACT.Identity,
                                       bias=par[:, h, 15:16]).then_inc(s["proj_read"], 1)
                        if h >= 1:
                            silu(h - 1)
                        if h % 4 == 2 and h > 4:
                            v_rows((h - 6) // 4)
                    silu(H - 1)
                    v_rows(HG - 1)
                    act.wait_ge(s["proj_read"], (i + 1) * H)
                    act.wait_ge(s["halo_out"], (i + 1) * H)
                    act.wait_ge(s["sums_ps"], (i + 1) * HG)
                    lo = Order(act, s["sp_log"], i * 12)
                    for n in range(HG):
                        lo.done(act.activation(sp_w[n], by_group(dec, n), ACT.Abs))
                    for n in range(HG):
                        lo.wait(n + 1)
                        lo.done(act.activation(sp_w[n], sp_w[n], ACT.Exp, scale=-1.0))
                    for n in range(HG):
                        lo.wait(HG + n + 1)
                        if n >= 2:
                            act.wait_ge(s["sp_sum"], i * HG + (n - 1))
                        lo.done(act.activation(sp_ln[n % 2], sp_w[n], ACT.Ln, bias=cst[:, K_ONE:K_ONE + 1]))
                    for n in range(HG):
                        act.wait_ge(s["sp_sum"], i * HG + (n + 1))
                        for h in range(HJ * n, HJ * n + HJ):
                            last = act.activation(by_head(dec, h), by_head(dec, h), ACT.Exp, scale=nega[:, h:h + 1])
                        last.then_inc(s["decay_ready"], 1)
                    act.wait_ge(s["sums_ps"], (i + 1) * HG)
                    act.activation(kap[:, :], ps[:, 6, 0:2 * NG], ACT.Sqrt,
                                   bias=cst[:, K_EPS6:K_EPS6 + 1]).then_inc(s["roots_ready"], 1)
                    act.wait_ge(s["beta_ps"], i + 1)
                    act.wait_ge(s["beta_out"], i * 16 * HG)
                    act.activation(beta[:, :], ps[0:H, 7, 0:TT], ACT.Sigmoid).then_inc(s["beta_ready"], 1)
                    act.wait_ge(s["kapt_ps"], i + 1)
                    act.activation(kapt[:, :], ps[0:NG, 6, 0:P], ACT.Copy).then_inc(s["kapt_ready"], 1)
                    act.wait_ge(s["tot_ready"], i + 1)
                    for n in range(NG // 4):
                        act.wait_ge(s["kkt_ps"], i * (NG // 4) + (n + 1))
                        for g in range(4 * n, 4 * n + 4):
                            last = act.activation(kkt[:, g, :], ps[:, n % 4, (g % 4) * P:(g % 4 + 1) * P], ACT.Copy,
                                                  scale=kap[:, g:g + 1])
                        last.then_inc(s["kkt_read"], 1)
                    for n in range(NG + 1):
                        if n < NG:
                            act.wait_ge(s["u_ps"], i * NG + (n + 1))
                            if n >= 2:
                                act.wait_ge(s["s_ps"], i * NG + (n - 1))
                                act.wait_ge(s["ubd_ready"], i * NG + (n - 1))
                            act.activation(ubuf[:, n % 2, :], ps[:, 4 + n % 2, 0:P], ACT.Copy).then_inc(s["u_ready"], 1)
                        if n >= 1:
                            m = n - 1
                            g = (m % HG) * NC_ + m // HG
                            act.wait_ge(s["o_ps"], i * NG + (m + 1))
                            act.activation(val[:, g, :], ps[:, 2 + m % 2, 0:P], ACT.Copy)
                            act.wait_ge(s["o_read"], i * NG + max(m - 1, 0))
                            act.activation(junk[:, m % 2, :], ps[:, 2 + m % 2, 0:P], ACT.Square,
                                           accum_out=oss[:, g:g + 1]).then_inc(s["o_read"], 1)
                    act.wait_ge(s["ofac_var"], i + 1)
                    act.activation(ofac[:, :], ofac[:, :], ACT.Sqrt, bias=cst[:, K_EPS5:K_EPS5 + 1]).then_inc(s["ofac_std"], 1)
                    for h in range(H):
                        act.wait_ge(s["gate_ps"], i * H + (h + 1))
                        if h >= 2:
                            act.wait_ge(s["ot_ready"], i * H + (h - 1))
                        act.activation(sg[h % 2], ps[:, h % 2, 0:TT], ACT.Sigmoid).then_inc(s["gate_ready"], 1)

            @block.vector
            def _(dve):
                dve.memset(state[:], 0.0).then_inc(s["dve_order"], 1)
                dve.wait_ge(s["dve_order"], 1)
                dve.wait_ge(s["const_ready"], 1)

                def carry(col):
                    dve.tensor_tensor(waited[:, col:col + 1], cst[:, K_ONE:K_ONE + 1], cst[:, K_ONE:K_ONE + 1], ALU.mult)

                with dve.Fori(0, TN, 1) as i:
                    o = Order(dve, s["dve_order"], i * DVE_PER_STEP + 1)
                    dve.wait_ge(s["y_ready"], i * 2)
                    for h in range(H):
                        b = h % 2
                        dve.wait_ge(s["proj_read"], i * H + (h + 1))
                        dve.wait_ge(s["halo_in"], i * H + (h + 1))
                        for tap in range(3):
                            for a in range(3):
                                if tap > 0:
                                    o.wait(o.n - 2)
                                ins = dve.scalar_tensor_tensor(cv[b][:, a], raw[b][:, a, tap:tap + TT],
                                                               par[:, h, 4 * a + tap:4 * a + tap + 1], cv[b][:, a],
                                                               ALU.mult, ALU.add)
                                if tap == 2 and a == 2:
                                    ins.then_inc(s["conv_done"], 1)
                                else:
                                    o.done(ins)
                    dve.wait_ge(s["v_ps"], (i + 1) * HG)
                    for n in range(HG):
                        dve.wait_ge(s["sp_log"], i * 12 + (HG + n + 1))
                        o.done(dve.tensor_scalar(sp_poly, sp_w[n], -0.25, None, ALU.mult))
                        for c in (1.0 / 3.0, -0.5, 1.0):
                            o.wait()
                            o.done(dve.scalar_tensor_tensor(sp_poly, sp_poly, c, sp_w[n], ALU.add, ALU.mult))
                        dve.wait_ge(s["sp_log"], i * 12 + (2 * HG + n + 1))
                        o.wait()
                        o.done(dve.tensor_scalar(sp_w[n], sp_w[n], 2.0 ** -6, None, ALU.is_lt))
                        o.wait()
                        carry(UNITS + n)
                        o.done(dve.copy_predicated(sp_ln[n % 2], sp_w[n].bitcast(I32), sp_poly))
                        o.wait()
                        dve.scalar_tensor_tensor(by_group(dec, n), by_group(dec, n), 0.0, sp_ln[n % 2],
                                                 ALU.max, ALU.add).then_inc(s["sp_sum"], 1)
                    for u in range(UNITS):
                        lv, half = u // 2, u % 2
                        m = 1 << max(lv - 1, 0)
                        gs = slice(half * NG // 2, (half + 1) * NG // 2)
                        dve.wait_ge(s["lvl_ps"], i * UNITS + (u + 1))
                        carry(u)
                        if lv == 0:
                            mask = cst[:, K_MASK:K_MASK + C].bitcast(I32).unsqueeze(1).broadcast_to([P, NG // 2, C])
                            dve.copy_predicated(amat[:, gs, 1, :], mask,
                                                ps[:, u % 4, :].rearrange("p (g t) -> p g t", t=C))
                            dve.wait_ge(s["decay_ready"], i * HG + (2 * half + 2))
                            dve.tensor_tensor(kq[:, 0, gs], kk[:, gs], dec[:, gs], ALU.mult)
                            dve.tensor_tensor(kq[:, 1, gs], kq[:, 1, gs], dec[:, gs],
                                              ALU.mult).then_inc(s["lvl_done"], 1)
                            continue
                        seg = C // (2 * m)
                        view = amat[:, gs, :, :].rearrange("p g w (e r m) -> p (g w) e r m", r=2, m=m)[:, :, :, 1, :]
                        mask = cst[:, K_MASK + 32 * lv:K_MASK + 32 * lv + C // 2].bitcast(I32).rearrange(
                            "p (e m) -> p e m", m=m).unsqueeze(1).broadcast_to([P, NG, seg, m])
                        dve.copy_predicated(view, mask, ps[:, u % 4, :].rearrange("p (g e m) -> p g e m", e=seg, m=m))
                        nb = H // 2 * TT // (2 * m)
                        cut = lambda ap: ap.rearrange("p g j t -> p (g j t)").rearrange("p (n r m) -> p n r m", r=2, m=m)
                        kkv, dv = cut(kk[:, gs]), cut(dec[:, gs])
                        left, right = dv[:, :, 0, 0:1], dv[:, :, 1, 0:1]
                        dve.wait_ge(s["lvl_done"], i * UNITS + (u - 1))
                        late = kq[:, :, gs].rearrange("p w g j t -> p w (g j t)").rearrange(
                            "p w (n r m) -> p w n r m", r=2, m=m)[:, :, :, 1, :]
                        o.done(dve.tensor_tensor(late, late, left.unsqueeze(1).broadcast_to([P, 2, nb, m]), ALU.mult))
                        early = kkv[:, :, 0, :]
                        o.done(dve.tensor_tensor(early, early, right.broadcast_to([P, nb, m]), ALU.mult))
                        o.wait()
                        dve.tensor_tensor(left, left, right, ALU.mult).then_inc(s["lvl_done"], 1)
                    dve.wait_ge(s["lvl_done"], (i + 1) * UNITS)
                    dve.tensor_copy(tot[:, :, :], dec[:, :, :, 0]).then_inc(s["tot_ready"], 1)
                    dve.wait_ge(s["roots_ready"], i + 1)
                    o.done(dve.reciprocal(kap[:, :], kap[:, :]))
                    o.wait()
                    dve.tensor_scalar(nkap[:, :], kap[:, 0:NG], -1.0, None, ALU.mult).then_inc(s["kap_ready"], 1)
                    dve.wait_ge(s["a_in"], (i + 1) * 16)
                    dve.wait_ge(s["beta_in"], (i + 1) * 16)
                    dve.wait_ge(s["kapt_in"], (i + 1) * 16)
                    dve.wait_ge(s["unit_in"], (i + 1) * 16)
                    block_ = [P, C, C]
                    o.done(dve.tensor_tensor(nm, nm, kb[:, :].unsqueeze(2).broadcast_to(block_), ALU.mult))
                    o.wait()
                    o.done(dve.tensor_tensor(kb[:, :], kb[:, :], bb[:, :], ALU.mult))
                    o.wait()
                    o.done(dve.tensor_tensor(nm, nm, kb[:, :].unsqueeze(1).broadcast_to(block_), ALU.mult))
                    for r in range(C - 1):
                        part = [P, r + 1, C - 1 - r]
                        o.wait()
                        o.done(dve.tensor_tensor(zt[:, 0:r + 1, r + 1:C], zm[:, 0:r + 1, r:r + 1].broadcast_to(part),
                                                 nm[:, r:r + 1, r + 1:C].broadcast_to(part), ALU.mult))
                        o.wait()
                        o.done(dve.tensor_tensor(zm[:, 0:r + 1, r + 1:C], zm[:, 0:r + 1, r + 1:C],
                                                 zt[:, 0:r + 1, r + 1:C], ALU.subtract))
                    o.wait()
                    dve.tensor_tensor(zm, zm, bb[:, :].unsqueeze(2).broadcast_to(block_), ALU.mult).then_inc(s["t_ready"], 1)
                    dve.wait_ge(s["v_rows"], (i + 1) * HG)
                    dve.wait_ge(s["kap_ready"], i + 1)
                    dve.wait_ge(s["tot_ready"], i + 1)
                    for n in range(NG + 2):
                        if n < NG:
                            g = (n % HG) * NC_ + n // HG
                            dve.wait_ge(s["kps"], i * NG + (n + 1))
                            if n >= 2:
                                dve.wait_ge(s["u_ps"], i * NG + (n - 1))
                            dve.scalar_tensor_tensor(rbuf[:, n % 2, :], ps[:, n % 2, 0:P], nkap[:, g:g + 1], val[:, g, :],
                                                     ALU.mult, ALU.add).then_inc(s["r_ready"], 1)
                        if 1 <= n <= NG:
                            m = n - 1
                            dve.wait_ge(s["u_ready"], i * NG + (m + 1))
                            if m >= 2:
                                dve.wait_ge(s["s_ps"], i * NG + (m - 1))
                            dve.tensor_tensor(ubd[:, m % 2], ubuf[:, m % 2, :].unsqueeze(1).broadcast_to([P, HJ, P]),
                                              cst[:, K_JM:K_JM + HJ].unsqueeze(2).broadcast_to([P, HJ, P]),
                                              ALU.mult).then_inc(s["ubd_ready"], 1)
                        if n >= 2:
                            m = n - 2
                            dve.wait_ge(s["s_ps"], i * NG + (m + 1))
                            dve.wait_ge(s["s_read"], i * NG + max(m - 3, 0))
                            for j in range(HJ):
                                h, g = (m % HG) * HJ + j, (m % HG) * NC_ + m // HG
                                last = dve.scalar_tensor_tensor(state[:, h, :], state[:, h, :],
                                                                tot[:, g, j:j + 1],
                                                                ps[:, 6 + m % 2, j * P:(j + 1) * P], ALU.mult, ALU.add)
                            last.then_inc(s["s_read"], 1)
                    dve.wait_ge(s["o_read"], (i + 1) * NG)
                    kapq = kap[:, NG:2 * NG]
                    o.done(dve.tensor_tensor(ofac[:, :], oss[:, :], kapq, ALU.mult))
                    o.wait()
                    dve.scalar_tensor_tensor(ofac[:, :], ofac[:, :], 1.0 / (P * P), kapq, ALU.mult,
                                             ALU.mult).then_inc(s["ofac_var"], 1)
                    dve.wait_ge(s["ofac_std"], i + 1)
                    o.done(dve.reciprocal(ofac[:, :], ofac[:, :]))
                    o.wait()
                    o.done(dve.scalar_tensor_tensor(ofac[:, :], ofac[:, :], float(P) ** -0.5, kapq, ALU.mult, ALU.mult))
                    o.wait()
                    for hg in range(HG):
                        gs = slice(hg * NC_, (hg + 1) * NC_)
                        dve.tensor_tensor(val[:, gs, :], val[:, gs, :], ofac[:, gs].unsqueeze(2).broadcast_to([P, NC_, P]),
                                          ALU.mult).then_inc(s["o_scaled"], 1)
                    for h in range(H):
                        hg, j = h // HJ, h % HJ
                        pair = 2 + 2 * (hg % 2)
                        dve.wait_ge(s["ot_ps"], i * HG + (hg + 1))
                        dve.wait_ge(s["gate_ready"], i * H + (h + 1))
                        o_t = ps[:, pair:pair + 2, :].rearrange("p b (c j t) -> p (b c) j t", j=HJ, t=C)[:, :, j, :]
                        dve.scalar_tensor_tensor(ot[:, h, :].rearrange("p (c t) -> p c t", t=C), o_t, onw[:, 0:1],
                                                 sg[h % 2].rearrange("p (c t) -> p c t", t=C),
                                                 ALU.mult, ALU.mult).then_inc(s["ot_ready"], 1)
                    dve.wait_ge(s["y_ps"], (i + 1) * (H // 2))
                    dve.wait_ge(s["x_loaded"], (i + 1) * 32)
                    for n in range(2):
                        dve.tensor_tensor(xio[:, n, :], ps[:, 6 + n, :], xio[:, n, :], ALU.add).then_inc(s["y_ready"], 1)
                    assert o.n == DVE_PER_STEP, o.n

            @block.tensor
            def _(pe):
                pe.wait_ge(s["setup"], 80)
                with pe.Fori(0, TN, 1) as i:
                    pe.wait_ge(s["y_ready"], i * 2)
                    pe.wait_ge(s["xt_in"], (i + 1) * 16)
                    for a in range(2):
                        for k in range(KC):
                            last = pe.matmul(ps[:, 4, a * TT:(a + 1) * TT], wab[:, k, a * P:(a + 1) * P], xt[:, k, :],
                                             start=(k == 0), stop=(k == KC - 1))
                        last.then_inc(s["fg_ps"], 1)
                    for k in range(KC):
                        last = pe.matmul(ps[0:H, 7, 0:TT], wab[:, k, 2 * P:2 * P + H], xt[:, k, :],
                                         start=(k == 0), stop=(k == KC - 1))
                    last.then_inc(s["beta_ps"], 1)
                    pe.wait_ge(s["fg_ready"], i + 1)

                    def group(hg):
                        pe.wait_ge(s["silu_done"], i * H + (HJ * hg + HJ))
                        pe.wait_ge(s["v_rows"], i * HG + hg)
                        for c in range(NC_):
                            last = pe.transpose(ps[:, 4 + c // 4, (c % 4) * P:(c % 4 + 1) * P],
                                                vt[:, c].rearrange("p j t -> p (j t)"), ident)
                        last.then_inc(s["v_ps"], 1)
                        pe.wait_ge(s["squared"], i * H + (HJ * hg + HJ))
                        for w in range(2):
                            for c in range(NC_):
                                col = w * NG + hg * NC_ + c
                                last = pe.matmul(ps[:, 6, col:col + 1], sq[:, w, c].rearrange("p j t -> p (j t)"),
                                                 cst[:, K_ONE:K_ONE + 1], start=True, stop=True)
                        last.then_inc(s["sums_ps"], 1)

                    for h in range(H):
                        b = h % 2
                        pe.wait_ge(w_in[b], (i * (H // 2) + (h // 2 + 1)) * 16)
                        if h >= 2:
                            pe.wait_ge(s["proj_read"], i * H + (h - 1))
                        for a in range(3):
                            for k in range(KC):
                                pe.matmul(ps[:, 2 * b + a // 2, (a % 2) * TT:(a % 2 + 1) * TT], wqkv[:, b, a, k, :],
                                          xt[:, k, :], start=(k == 0), stop=(k == KC - 1))
                        pe.matmul(ps[:, 2 * b + 1, TT:2 * TT], wfb[:, h * P:(h + 1) * P], fg[:, 0, :],
                                  start=True, stop=True).then_inc(s["proj_ps"], 1)
                        if h % HJ == 1 and h > HJ:
                            group((h - 5) // HJ)
                    group(HG - 1)

                    pe.wait_ge(s["proj_read"], (i + 1) * H)
                    for u in range(UNITS):
                        lv, half = u // 2, u % 2
                        m = 1 << max(lv - 1, 0)
                        if lv > 0:
                            pe.wait_ge(s["lvl_done"], i * UNITS + (u - 1))
                        for g in range(half * NG // 2, (half + 1) * NG // 2):
                            n = g % (NG // 2)
                            for j in range(HJ):
                                if lv == 0:
                                    rhs = kq[:, 1, g, j, :]
                                else:
                                    rhs = kq[:, :, g, j, :].rearrange("p w (e r m) -> p w e r m", r=2, m=m)[:, :, :, 1, :]
                                last = pe.matmul(ps[C * j:C * j + C, u % 4, n * C:(n + 1) * C], kk[:, g, j, :], rhs,
                                                 start=True, stop=True)
                        last.then_inc(s["lvl_ps"], 1)
                    pe.wait_ge(s["lvl_done"], (i + 1) * UNITS)
                    for n in range(NG // 4):
                        if n >= 4:
                            pe.wait_ge(s["kkt_read"], i * (NG // 4) + (n - 3))
                        for g in range(4 * n, 4 * n + 4):
                            last = pe.transpose(ps[:, n % 4, (g % 4) * P:(g % 4 + 1) * P],
                                                kk[:, g].rearrange("p j t -> p (j t)"), ident)
                        last.then_inc(s["kkt_ps"], 1)
                        if n == 3:
                            pe.wait_ge(s["kap_ready"], i + 1)
                            pe.transpose(ps[0:NG, 6, 0:P], kap[:, 0:NG], ident).then_inc(s["kapt_ps"], 1)
                    pe.wait_ge(s["kkt_read"], (i + 1) * (NG // 4))
                    pe.wait_ge(s["kapt_ready"], i + 1)
                    for n in range(NG + 2):
                        if n < NG:
                            hg, c, b = n % HG, n // HG, n % 2
                            pe.wait_ge(s["s_read"], i * NG + max(n - 3, 0))
                            if n >= 2:
                                pe.wait_ge(s["r_ready"], i * NG + (n - 1))
                            for j in range(HJ):
                                last = pe.matmul(ps[C * j:C * j + C, b, 0:P], kq[:, 0, hg * NC_ + c, j, :],
                                                 state[:, HJ * hg + j, :], start=True, stop=True)
                            last.then_inc(s["kps"], 1)
                        if 1 <= n <= NG:
                            m = n - 1
                            g = (m % HG) * NC_ + m // HG
                            if m >= 2:
                                pe.wait_ge(s["o_read"], i * NG + (m - 1))
                            for j in range(HJ):
                                pe.matmul(ps[C * j:C * j + C, 2 + m % 2, 0:P], kq[:, 1, g, j, :],
                                          state[:, m % HG * HJ + j, :], start=True, stop=False, skip_group_check=True)
                            if m == 0:
                                pe.wait_ge(s["t_in"], (i + 1) * 16 * HJ)
                            pe.wait_ge(s["r_ready"], i * NG + (m + 1))
                            if m >= 2:
                                pe.wait_ge(s["u_ready"], i * NG + (m - 1))
                            pe.matmul(ps[:, 4 + m % 2, 0:P], bdt[:, g].rearrange("p j t -> p (j t)"), rbuf[:, m % 2, :],
                                      start=True, stop=True).then_inc(s["u_ps"], 1)
                        if n >= 2:
                            m = n - 2
                            g = (m % HG) * NC_ + m // HG
                            if m == 0:
                                pe.wait_ge(s["bda_ready"], (i + 1) * HJ)
                            pe.wait_ge(s["ubd_ready"], i * NG + (m + 1))
                            pe.matmul(ps[:, 2 + m % 2, 0:P], bda[:, g].rearrange("p j t -> p (j t)"), ubuf[:, m % 2, :],
                                      start=False, stop=True, skip_group_check=True).then_inc(s["o_ps"], 1)
                            if m >= 2:
                                pe.wait_ge(s["s_read"], i * NG + (m - 1))
                            pe.matmul(ps[:, 6 + m % 2, :], kkt[:, g, :], ubd[:, m % 2].rearrange("p j v -> p (j v)"),
                                      start=True, stop=True).then_inc(s["s_ps"], 1)

                    def out_rows(n):
                        pe.wait_ge(wo_in[n % 2], (i * (H // 4) + (n // 2 + 1)) * 16)
                        pe.wait_ge(s["ot_ready"], i * H + (2 * n + 2))
                        for h in (2 * n, 2 * n + 1):
                            for k in range(2):
                                last = pe.matmul(ps[:, 6 + k, :], ot[:, h, k * P:(k + 1) * P], wo[n % 2][:, h % 2, :],
                                                 start=(h == 0), stop=(h == H - 1))
                        last.then_inc(s["y_ps"], 1)

                    pe.wait_ge(s["s_read"], (i + 1) * NG)
                    for hg in range(HG):
                        pe.wait_ge(s["o_scaled"], i * HG + (hg + 1))
                        if hg >= 2:
                            pe.wait_ge(s["ot_ready"], i * H + (hg - 1) * HJ)
                        for c in range(NC_):
                            last = pe.transpose(ps[:, 2 + 2 * (hg % 2) + c // 4, (c % 4) * P:(c % 4 + 1) * P],
                                                val[:, hg * NC_ + c, :], ident)
                        last.then_inc(s["ot_ps"], 1)
                        for h in range(HJ * hg, HJ * hg + HJ):
                            if h >= 2:
                                pe.wait_ge(s["gate_ready"], i * H + (h - 1))
                                pe.wait_ge(s["ot_ready"], i * H + max(h - 3, 0))
                            pe.matmul(ps[:, h % 2, 0:TT], wgb[:, h * P:(h + 1) * P], fg[:, 1, :],
                                      start=True, stop=True).then_inc(s["gate_ps"], 1)
                        if hg > 0:
                            out_rows(2 * hg - 2)
                            out_rows(2 * hg - 1)
                    out_rows(H // 2 - 2)
                    out_rows(H // 2 - 1)


def program(nc, d, out, until=9):
    with ExitStack() as ctx:
        sem = lambda n: ctx.enter_context(nc.semaphore(n))
        ps = ctx.enter_context(nc.psum_tensor("psum", [P, 8, 512], F32))
        cst = ctx.enter_context(nc.sbuf_tensor("constants_sb", [P, K_N], F32))
        x1 = nc.dram_tensor("x_after_attention", [T, D], F32).ap()
        x2 = nc.dram_tensor("x_after_experts", [T, D], F32).ap()
        x3 = nc.dram_tensor("x_after_delta", [T, D], F32).ap()
        xnt_dram = nc.dram_tensor("xn_transposed", [TN, P, KC, TT], F32).ap()

        def load(x_sb, source, name, with_constants=False):
            loaded = sem(name)
            with nc.Block() as block:
                @block.sync
                def _(sp):
                    sp.dma_start(x_sb[:, :, :], source.rearrange("(n p) d -> p n d", p=P)).then_inc(loaded, 16)
                    if with_constants:
                        sp.dma_start(cst[:, :], d["constants"]).then_inc(loaded, 16)
                    sp.wait_ge(loaded, 32 if with_constants else 16)

        with ExitStack() as c2:
            x_sb = c2.enter_context(nc.sbuf_tensor("x1_sb", [P, NT, D], F32))
            xnt = c2.enter_context(nc.sbuf_tensor("xnt1_sb", [P, KC, T], F32))
            load(x_sb, d["x"], "x_loaded", True)
            norm_stage(nc, "n1_", x_sb, xnt, ps, cst, gram=True)
            attention_stage(nc, x_sb, xnt, ps, cst, d)
            norm_stage(nc, "n2_", x_sb, xnt, ps, cst)
            ffn_stage(nc, "f1_", x_sb, xnt, ps, cst, d, x2 if until > 1 else out)
            if until == 1:
                return
            norm_stage(nc, "n3_", x_sb, xnt, ps, cst)
            stored = sem("xnt_stored")
            with nc.Block() as block:
                @block.sync
                def _(sp):
                    for i in range(TN):
                        sp.dma_start(xnt_dram[i], xnt[:, :, i * TT:(i + 1) * TT]).then_inc(stored, 16)
                    sp.wait_ge(stored, 16 * TN)
        delta_stage(nc, x2, x3 if until > 2 else out, xnt_dram, ps, cst, d)
        if until == 2:
            return
        with ExitStack() as c2:
            x_sb = c2.enter_context(nc.sbuf_tensor("x3_sb", [P, NT, D], F32))
            xnt = c2.enter_context(nc.sbuf_tensor("xnt3_sb", [P, KC, T], F32))
            load(x_sb, x3, "x3_loaded")
            norm_stage(nc, "n4_", x_sb, xnt, ps, cst)
            ffn_stage(nc, "f2_", x_sb, xnt, ps, cst, d, out)


def arrange(inputs):
    import numpy as np
    f = {k.split("L0_")[1]: np.asarray(v) for k, v in inputs.items()}
    rows = lambda a, k: a.reshape(k, P, -1).transpose(1, 0, 2)
    d = {"constants": constants(), "x": f["attn_a_x"][0]}
    d["select"] = np.repeat(np.eye(NE, NR, dtype=np.float32)[:, :, None], P, 2)
    d["unit"] = np.broadcast_to(np.eye(C, dtype=np.float32), (P, C, C))
    d["wq"], d["wk"], d["wo"] = f["attn_a_Wq"], f["attn_a_Wk"], f["attn_a_Wo"]
    d["wvt"] = f["attn_a_Wv"].T
    d["router"] = rows(f["ffn_Wg"], KC)
    d["brouter"] = np.broadcast_to(f["ffn_bg"], (P, NE))
    d["wgate"] = f["ffn_Wgate"].reshape(NR, KC, P, FH).transpose(2, 0, 1, 3)
    d["wup"] = f["ffn_Wup"].reshape(NR, KC, P, FH).transpose(2, 0, 1, 3)
    d["wdown"] = f["ffn_Wdown"].reshape(NR, HC, P, D).transpose(2, 0, 1, 3)
    d["wsup"], d["wsdown"] = rows(f["ffn_Ws_up"], KC), rows(f["ffn_Ws_down"], SC)
    d["bgate"] = f["ffn_bgate"].reshape(NR * HC, P).T
    d["bup"] = f["ffn_bup"].reshape(NR * HC, P).T
    d["bsup"] = f["ffn_bs_up"].reshape(SC, P).T
    d["bdown"] = np.concatenate([f["ffn_bdown"], f["ffn_bs_down"][None]])
    heads = lambda a: a.reshape(KC, P, H, P).transpose(2, 1, 0, 3)
    d["dw_qkv"] = np.stack([heads(f["attn_b_Wq"]), heads(f["attn_b_Wk"]), heads(f["attn_b_Wv"])], 2)
    per = [f[f"attn_b_conv_{n}_w"].reshape(H, P, 4).transpose(1, 0, 2) for n in "qkv"]
    per += [f[f"attn_b_conv_{n}_b"].reshape(H, P, 1).transpose(1, 0, 2) for n in "qkv"]
    per += [f["attn_b_dt_bias"].reshape(H, P, 1).transpose(1, 0, 2)]
    per += [np.broadcast_to(f["attn_b_A_log"][None, :, None], (P, H, 1))]
    d["dheads"] = np.concatenate(per, 2)
    d["dwa"] = np.concatenate([rows(f["attn_b_Wfa"], KC), rows(f["attn_b_Wga"], KC), rows(f["attn_b_Wb"], KC)], 2)
    d["dwfb"], d["dwgb"] = f["attn_b_Wfb"], f["attn_b_Wgb"]
    d["donorm"] = f["attn_b_o_norm_w"].reshape(P, 1)
    d["dwo"] = f["attn_b_Wo"].reshape(H // 2, 2, P, D).transpose(0, 2, 1, 3)
    return {k: np.ascontiguousarray(v) for k, v in d.items()}


def kernel(**inputs):
    import numpy as np
    import concourse.bacc as bacc
    from concourse.bass_utils import run_bass_kernel_spmd

    arrays = arrange(inputs)
    nc = bacc.Bacc("TRN2", target_bir_lowering=False, num_devices=1)
    d = {n: nc.dram_tensor("in_" + n, a.shape, mybir.dt.from_np(a.dtype), kind="ExternalInput").ap()
         for n, a in arrays.items()}
    out = nc.dram_tensor("out", (T, D), F32, kind="ExternalOutput").ap()
    program(nc, d, out)
    r = run_bass_kernel_spmd(nc, [{"in_" + n: a for n, a in arrays.items()}], core_ids=[0])
    return r.results[0]["out"].reshape(1, T, D)
```

```python
from contextlib import ExitStack, contextmanager

import concourse.bass as bass
from concourse import mybir

F32 = mybir.dt.float32
I32 = mybir.dt.int32
ALU = mybir.AluOpType
ACT = mybir.ActivationFunctionType
AX = mybir.AxisListType

P = 128
T = 2048
D = 512
NT = T // P
KC = D // P
EPS = 1e-5

NR = 6
NE = 8
FH = 256
HC = FH // P
SC = D // P
FT = 512
FN = T // FT

H = 16
HG = 4
HJ = 4
C = 32
TT = 256
TN = T // TT
NC_ = TT // C
NG = HG * NC_
LEVELS = 5
KEPS = 1e-6
LEVELS1 = LEVELS + 1
GH = NG // 2
DVE_PER_STEP = 222
POOL_PER_STEP = 130
KKT_BANK = ((0, 1, 2, 3), (4, 5, 4, 5))
L_BANK = (7, 5)
O_BANK = (2, 5)
PARTS = (("head", 0), ("gate", 2, 0), ("head", 1), ("gate", 2, 1), ("head", 2), ("gate", 3, 0), ("head", 3),
         ("gate", 3, 1), ("head", 4), ("head", 5))

K_ID, K_ONE, K_JM, K_MASK, K_EPS5, K_EPS6, K_JLT = 0, 128, 256, 260, 452, 453, 454
K_N = 518


def constants():
    import numpy as np
    c = np.zeros((P, K_N), np.float32)
    p = np.arange(P)
    c[:, K_ID:K_ID + P] = np.eye(P)
    c[:, K_ONE:K_ONE + P] = 1.0
    c[p, K_JM + p // C] = 1.0
    s = p % C
    for t in range(C):
        c[s == t, K_MASK + t] = 1.0
    for lv in range(1, LEVELS + 1):
        m = 1 << (lv - 1)
        for n in range(C // 2):
            seg, k = n // m, n % m
            ok = (s // (2 * m) == seg) & (s % (2 * m) < m)
            c[ok, K_MASK + 32 * lv + n] = 1.0
    c[:, K_EPS5] = EPS
    c[:, K_EPS6] = KEPS
    for i in range(NE):
        for j in range(i):
            c[:, K_JLT + i * NE + j] = 1.0
    return c


class Order:

    def __init__(self, eng, sem, base=0):
        self.eng, self.sem, self.base, self.n = eng, sem, base, 0

    def done(self, ins):
        ins.then_inc(self.sem, 1)
        self.n += 1
        return self.n

    def wait(self, n=None):
        self.eng.wait_ge(self.sem, self.base + (self.n if n is None else n))


@contextmanager
def stage_semaphores(nc):
    used = []

    def sem(name):
        used.append(nc.alloc_semaphore(name=name))
        return used[-1]
    yield sem
    nc.clear_and_free_semaphores(used)
    nc.all_engine_barrier()


def norm_stage(nc, tag, x_sb, xnt, ps, cst, gram=False, source=None, constants_from=None, ahead=None, store_to=None):
    with ExitStack() as c2:
        sem = c2.enter_context(stage_semaphores(nc))
        sb = lambda n, s: c2.enter_context(nc.sbuf_tensor(tag + n, s, F32))
        st = sb("stats", [P, NT, 6])
        mv = sb("meanvar", [P, NT, 2])
        rstd = sb("rstd", [P, NT])
        shift = sb("shift", [P, NT])
        xn = sb("xn", [P, 2, D])
        order = sem(tag + "dve_order")
        var_ready = sem(tag + "var_ready")
        std_ready = sem(tag + "std_ready")
        xn_ready = [sem(tag + f"xn_ready{b}") for b in range(2)]
        xn_read = [sem(tag + f"xn_read{b}") for b in range(2)]
        bank_free = [sem(tag + f"bank_free{b}") for b in range(2)]
        x_in = [sem(tag + f"x_in{q}") for q in range(4)]
        const_in = sem(tag + "const_in")
        stored = sem(tag + "stored")
        with nc.Block() as block:

            @block.sync
            def _(sp):
                if constants_from is not None:
                    sp.dma_start(cst[:, :], constants_from).then_inc(const_in, 16)
                if source is not None:
                    for q in range(4):
                        sp.dma_start(x_sb[:, 4 * q:4 * q + 4, :],
                                     source.rearrange("(n p) d -> p n d", p=P)[:, 4 * q:4 * q + 4, :]).then_inc(x_in[q], 16)
                if ahead is not None:
                    ahead(sp)
                if store_to is not None:
                    for i in range(TN):
                        for b in range(2):
                            sp.wait_ge(bank_free[b], i + 1)
                        sp.dma_start(store_to[i], xnt[:, :, i * TT:(i + 1) * TT]).then_inc(stored, 16)
                    sp.dma_start(store_to[TN], xnt[:, :, 0:TT]).then_inc(stored, 16)
                    sp.wait_ge(stored, 16 * (TN + 1))

            @block.vector
            def _(dve):
                o = Order(dve, order)
                for i in range(NT):
                    if source is not None and i % 4 == 0:
                        dve.wait_ge(x_in[i // 4], 16)
                    o.done(dve.bn_stats(st[:, i, :], x_sb[:, i, :]))
                o.wait()
                for i in range(NT):
                    last = dve.bn_aggr(mv[:, i, :], st[:, i, :])
                last.then_inc(var_ready, 1)
                dve.wait_ge(std_ready, 1)
                o.done(dve.reciprocal(rstd[:, :], rstd[:, :]))
                o.wait()
                o.done(dve.scalar_tensor_tensor(shift[:, :], mv[:, :, 0], -1.0, rstd[:, :], ALU.mult, ALU.mult))
                o.wait()
                for b in range(2):
                    dve.tensor_scalar(xn[:, b, :], x_sb[:, b, :], rstd[:, b:b + 1], shift[:, b:b + 1],
                                      ALU.mult, ALU.add).then_inc(xn_ready[b], 1)
                with dve.Fori(1, NT // 2, 1) as ii:
                    for b in range(2):
                        i = ii * 2 + b
                        dve.wait_ge(xn_read[b], ii)
                        dve.tensor_scalar(xn[:, b, :], x_sb[:, i, :], rstd[:, bass.ds(i, 1)], shift[:, bass.ds(i, 1)],
                                          ALU.mult, ALU.add).then_inc(xn_ready[b], 1)

            @block.scalar
            def _(act):
                if constants_from is not None:
                    act.wait_ge(const_in, 16)
                act.wait_ge(var_ready, 1)
                act.activation(rstd[:, :], mv[:, :, 1], ACT.Sqrt, bias=cst[:, K_EPS5:K_EPS5 + 1]).then_inc(std_ready, 1)
                with act.Fori(0, NT // 2, 1) as ii:
                    for b in range(2):
                        i = ii * 2 + b
                        act.wait_ge(xn_read[b], ii + 1)
                        act.activation(xnt[:, :, bass.ds(i * P, P)],
                                       ps[:, b, :].rearrange("p (k t) -> p k t", k=KC), ACT.Copy).then_inc(bank_free[b], 1)

            @block.tensor
            def _(pe):
                def tile(ii, first):
                    for b in range(2):
                        pe.wait_ge(xn_ready[b], ii + 1)
                        if gram:
                            for e in range(KC):
                                pe.matmul(ps[:, 4 + e, :], xn[:, b, e * P:(e + 1) * P], xn[:, b, :],
                                          start=(first and b == 0), stop=True, skip_group_check=True)
                        if not first:
                            pe.wait_ge(bank_free[b], ii)
                        for k in range(KC):
                            last = pe.transpose(ps[:, b, k * P:(k + 1) * P], xn[:, b, k * P:(k + 1) * P],
                                                cst[:, K_ID:K_ID + P])
                        last.then_inc(xn_read[b], 1)
                if constants_from is not None:
                    pe.wait_ge(const_in, 16)
                tile(0, True)
                with pe.Fori(1, NT // 2, 1) as ii:
                    tile(ii, False)


def attention_stage(nc, x_sb, xnt, ps, cst, dram, ahead):
    with ExitStack() as c2:
        sem = c2.enter_context(stage_semaphores(nc))
        sb = lambda n, s: c2.enter_context(nc.sbuf_tensor("at_" + n, s, F32))
        w = {n: sb(n, [P, KC, D]) for n in ("wq", "wk", "wo", "wvt")}
        g, t1, pr, r1, m = (sb(n, [P, KC, D]) for n in ("g", "t1", "pr", "r1", "m"))
        mx, nmx, rs, rc = (sb(n, [P, KC]) for n in ("mx", "nmx", "rs", "rc"))
        w_in = {n: sem("at_in_" + n) for n in w}
        g_ready, t1_ps, t1_ready, s_ps, neg_max, exp_ready, p_ready, r1_ps, r1_ready, m_ps, m_ready, order = (
            sem("at_" + n) for n in ("g_ready", "t1_ps", "t1_ready", "s_ps", "neg_max", "exp_ready", "p_ready",
                                     "r1_ps", "r1_ready", "m_ps", "m_ready", "order"))
        y_ps = [sem(f"at_y_ps{b}") for b in range(4)]
        y_read = [sem(f"at_y_read{b}") for b in range(4)]
        with nc.Block() as block:

            @block.sync
            def _(sp):
                for n in ("wk", "wq", "wo", "wvt"):
                    sp.dma_start(w[n][:, :, :], dram[n].rearrange("(k p) n -> p k n", p=P)).then_inc(w_in[n], 16)
                ahead(sp)

            @block.tensor
            def _(pe):
                def product(banks, lhs, rhs, signal):
                    for e in range(KC):
                        for k in range(KC):
                            last = pe.matmul(ps[:, banks + e, :], lhs[:, k, e * P:(e + 1) * P], rhs[:, k, :],
                                             start=(k == 0), stop=(k == KC - 1))
                        last.then_inc(signal, 1)
                pe.wait_ge(w_in["wk"], 16)
                pe.wait_ge(g_ready, KC)
                product(0, g, w["wk"], t1_ps)
                pe.wait_ge(w_in["wq"], 16)
                pe.wait_ge(t1_ready, KC)
                product(4, w["wq"], t1, s_ps)
                pe.wait_ge(w_in["wo"], 16)
                pe.wait_ge(p_ready, KC)
                product(0, pr, w["wo"], r1_ps)
                pe.wait_ge(w_in["wvt"], 16)
                pe.wait_ge(r1_ready, KC)
                product(4, w["wvt"], r1, m_ps)
                pe.wait_ge(m_ready, KC)
                for i in range(NT):
                    b = i % 4
                    if i >= 4:
                        pe.wait_ge(y_read[b], i // 4)
                    for k in range(KC):
                        last = pe.matmul(ps[:, b, :], xnt[:, k, i * P:(i + 1) * P], m[:, k, :],
                                         start=(k == 0), stop=(k == KC - 1))
                    last.then_inc(y_ps[b], 1)

            @block.scalar
            def _(act):
                for e in range(KC):
                    act.activation(g[:, e, :], ps[:, 4 + e, :], ACT.Copy).then_inc(g_ready, 1)
                for e in range(KC):
                    act.wait_ge(t1_ps, e + 1)
                    act.activation(t1[:, e, :], ps[:, e, :], ACT.Copy).then_inc(t1_ready, 1)
                for e in range(KC):
                    act.wait_ge(neg_max, e + 1)
                    act.activation(pr[:, e, :], ps[:, 4 + e, :], ACT.Exp, bias=nmx[:, e:e + 1], scale=0.25,
                                   accum_out=rs[:, e:e + 1]).then_inc(exp_ready, 1)
                for e in range(KC):
                    act.wait_ge(r1_ps, e + 1)
                    act.activation(r1[:, e, :], ps[:, e, :], ACT.Copy).then_inc(r1_ready, 1)
                for e in range(KC):
                    act.wait_ge(m_ps, e + 1)
                    act.activation(m[:, e, :], ps[:, 4 + e, :], ACT.Copy).then_inc(m_ready, 1)

            @block.vector
            def _(dve):
                o = Order(dve, order)
                for e in range(KC):
                    dve.wait_ge(s_ps, e + 1)
                    o.done(dve.reduce_max(mx[:, e:e + 1], ps[:, 4 + e, :], AX.X))
                    o.wait()
                    dve.tensor_scalar(nmx[:, e:e + 1], mx[:, e:e + 1], -0.25, None, ALU.mult).then_inc(neg_max, 1)
                for e in range(KC):
                    dve.wait_ge(exp_ready, e + 1)
                    o.done(dve.reciprocal(rc[:, e:e + 1], rs[:, e:e + 1]))
                    o.wait()
                    dve.tensor_scalar(pr[:, e, :], pr[:, e, :], rc[:, e:e + 1], None, ALU.mult).then_inc(p_ready, 1)
                for i in range(NT):
                    b = i % 4
                    dve.wait_ge(y_ps[b], i // 4 + 1)
                    dve.tensor_tensor(x_sb[:, i, :], ps[:, b, :], x_sb[:, i, :], ALU.add).then_inc(y_read[b], 1)


def ffn_stage(nc, tag, x_sb, xnt, ps, cst, dram, store_to, wg, wu, wgu_in):
    with ExitStack() as c2:
        sem = c2.enter_context(stage_semaphores(nc))
        sb = lambda n, s: c2.enter_context(nc.sbuf_tensor(tag + n, s, F32))
        wd = sb("wdown", [P, NR, HC, D])
        wsu = sb("wsup", [P, KC, D])
        wsd = sb("wsdown", [P, SC, D])
        wr = sb("wrouter", [P, KC, NE])
        br = sb("brouter", [P, NE])
        bg = sb("bgate", [P, NR * HC])
        bu = sb("bup", [P, NR * HC])
        bs = sb("bshared", [P, SC])
        bd = sb("bdown", [NR + 1, D])
        sel = sb("select", [NE, NR, P])
        wt = sb("weights_t", [NE, T])
        wts = sb("weights_t_step", [NE, FT])
        wb = sb("weights_b", [P, NR, FT])
        act_g = sb("act_g", [P, 2, FT])
        hid = sb("hidden", [P, 2, FT])
        lg = sb("logits", [P, NT, NE])
        pw = sb("probs", [P, NT, NE])
        mxl = sb("max", [P, NT])
        sm = sb("sum", [P, NT])
        cmp_a = act_g[:, :, :].rearrange("p a (b c d) -> p (a b) c d", c=NE, d=NE)
        cmp_b = hid[:, :, :].rearrange("p a (b c d) -> p (a b) c d", c=NE, d=NE)
        names = ("w_in", "wr_in", "wd_in", "wsh_in", "order", "logits_ps", "logits_max", "exp_ready", "probs_ready", "wt_ps",
                 "wt_ready", "acc_ps", "acc_read", "stored", "wts_ready", "bcast_ps", "bcast_ready", "step_read")
        (w_in, wr_in, wd_in, wsh_in, order, logits_ps, logits_max, exp_ready, probs_ready, wt_ps, wt_ready, acc_ps,
         acc_read, stored, wts_ready, bcast_ps, bcast_ready, step_read) = (sem(tag + n) for n in names)
        up_ps, gate_ready, hid_ready, hid_read = ([sem(tag + f"{n}{b}") for b in range(2)]
                                                  for n in ("up_ps", "gate_ready", "hid_ready", "hid_read"))
        units = [(n, c) for n in range(NR) for c in range(HC)] + [(NR, c) for c in range(SC)]
        NU = len(units)
        per_slot = NU // 2
        x_dram = store_to.rearrange("(n p) d -> n p d", p=P)
        with nc.Block() as block:

            @block.sync
            def _(sp):
                sp.dma_start(wr[:, :, :], dram["router"]).then_inc(wr_in, 16)
                sp.dma_start(br[:, :], dram["brouter"]).then_inc(wr_in, 16)
                for dst, name in ((bg, "bgate"), (bu, "bup"), (bs, "bsup"), (bd, "bdown"), (sel, "select")):
                    sp.dma_start(dst[:], dram[name]).then_inc(w_in, 16)
                sp.dma_start(wd[:], dram["wdown"]).then_inc(wd_in, 16)
                sp.dma_start(wsu[:], dram["wsup"]).then_inc(wsh_in, 16)
                sp.dma_start(wsd[:], dram["wsdown"]).then_inc(wsh_in, 16)
                with sp.Fori(0, FN, 1) as s:
                    sp.wait_ge(acc_read, s * 4 + 5)
                    for i in range(4):
                        sp.dma_start(x_dram[s * 4 + i], x_sb[:, s * 4 + i, :]).then_inc(stored, 16)
                sp.wait_ge(stored, 16 * NT)

            @block.tensor
            def _(pe):
                pe.wait_ge(wr_in, 32)
                for i in range(NT):
                    for k in range(KC):
                        last = pe.matmul(ps[:, 0, i * NE:(i + 1) * NE], xnt[:, k, i * P:(i + 1) * P], wr[:, k, :],
                                         start=(k == 0), stop=(k == KC - 1))
                last.then_inc(logits_ps, 1)
                pe.wait_ge(probs_ready, 1)
                for i in range(NT):
                    last = pe.transpose(ps[0:NE, 4 + i // 4, (i % 4) * P:(i % 4 + 1) * P], pw[:, i, :],
                                        cst[:, K_ID:K_ID + P])
                    if i < 3:
                        last.then_inc((hid_read[0], hid_read[1], acc_ps)[i], 1)
                last.then_inc(wt_ps, 1)
                pe.wait_ge(w_in, 16 * 5)
                with pe.Fori(0, FN, 1) as s:
                    pe.wait_ge(wts_ready, s + 1)
                    for n in range(NR):
                        if n >= 4:
                            pe.wait_ge(bcast_ready, s * NR + n - 3)
                        if n == 0:
                            pe.wait_ge(hid_ready[0], s * per_slot + 1)
                            pe.wait_ge(hid_ready[1], s * per_slot + 1)
                        last = pe.matmul(ps[:, n % 4, :], sel[:, n, :], wts[:, :],
                                         start=True, stop=True)
                        last.then_inc(bcast_ps, 1)
                    pe.wait_ge(bcast_ready, s * NR + NR)

                    def up(u):
                        n, c = units[u]
                        b = u % 2
                        if u == 0:
                            pe.wait_ge(wgu_in, 16 * 2)
                        if n == NR and c == 0:
                            pe.wait_ge(wsh_in, 16 * 2)
                        pe.wait_ge(hid_ready[b], s * per_slot + 1 + u // 2)
                        for k in range(KC):
                            lhs = wg[:, n, k, c * P:(c + 1) * P] if n < NR else wsu[:, k, c * P:(c + 1) * P]
                            last = pe.matmul(ps[:, 2 * b, :], lhs, xnt[:, k, bass.ds(s * FT, FT)],
                                             start=(k == 0), stop=(k == KC - 1))
                        if n < NR:
                            for k in range(KC):
                                last = pe.matmul(ps[:, 2 * b + 1, :], wu[:, n, k, c * P:(c + 1) * P],
                                                 xnt[:, k, bass.ds(s * FT, FT)], start=(k == 0), stop=(k == KC - 1))
                        last.then_inc(up_ps[b], 1)

                    def down(u):
                        n, c = units[u]
                        b = u % 2
                        pe.wait_ge(hid_ready[b], s * per_slot + 1 + (u // 2 + 1))
                        if u == 0:
                            pe.wait_ge(wd_in, 16)
                            pe.wait_ge(acc_read, s * 4 + 1)
                        for i in range(4):
                            rhs = wd[:, n, c, :] if n < NR else wsd[:, c, :]
                            last = pe.matmul(ps[:, 4 + i, :], hid[:, b, i * P:(i + 1) * P], rhs,
                                             start=(u == 0), stop=False)
                        last.then_inc(hid_read[b], 1)

                    up(0)
                    for u in range(1, NU):
                        up(u)
                        down(u - 1)
                    down(NU - 1)
                    for i in range(4):
                        last = pe.matmul(ps[:, 4 + i, :], wts[0:NR + 1, i * P:(i + 1) * P], bd[:, :],
                                         start=False, stop=True)
                    last.then_inc(acc_ps, 1)

            @block.scalar
            def _(act):
                act.wait_ge(logits_max, 1)
                act.activation(pw[:, :, :], lg[:, :, :], ACT.Exp).then_inc(exp_ready, 1)
                with act.Fori(0, FN, 1) as s:
                    for n in range(NR):
                        act.wait_ge(bcast_ps, s * NR + n + 1)
                        act.activation(wb[:, n, :], ps[:, n % 4, :], ACT.Copy).then_inc(bcast_ready, 1)
                    for u in range(NU):
                        n, c = units[u]
                        b = u % 2
                        act.wait_ge(up_ps[b], s * per_slot + (u // 2 + 1))
                        if n < NR:
                            act.wait_ge(hid_ready[b], s * per_slot + 1 + u // 2)
                            act.activation(act_g[:, b, :], ps[:, 2 * b, :], ACT.Silu,
                                           bias=bg[:, n * HC + c:n * HC + c + 1]).then_inc(gate_ready[b], 1)
                        else:
                            act.wait_ge(hid_read[b], s * per_slot + 1 + u // 2)
                            act.activation(hid[:, b, :], ps[:, 2 * b, :], ACT.Silu,
                                           bias=bs[:, c:c + 1]).then_inc(hid_ready[b], 1)

            @block.vector
            def _(dve):
                o = Order(dve, order)
                step = lambda ins: (o.done(ins), o.wait())
                dve.wait_ge(wr_in, 32)
                dve.wait_ge(logits_ps, 1)
                lgp = ps[:, 0, 0:NT * NE].rearrange("p (i e) -> p i e", e=NE)
                for n, started in enumerate((hid_ready[0], hid_ready[1], acc_read)):
                    dve.tensor_copy(wts[0:1, n:n + 1], cst[0:1, K_ONE:K_ONE + 1]).then_inc(started, 1)
                step(dve.tensor_tensor(lg[:, :, :], lgp, br[:, :].unsqueeze(1).broadcast_to([P, NT, NE]), ALU.add))
                step(dve.tensor_reduce(mxl[:, :], lg[:, :, :], AX.X, ALU.max))
                row = lg[:, :, :].unsqueeze(3).broadcast_to([P, NT, NE, NE])
                col = lg[:, :, :].unsqueeze(2).broadcast_to([P, NT, NE, NE])
                earlier = cst[:, K_JLT:K_JLT + NE * NE].rearrange("p (c d) -> p c d", c=NE).unsqueeze(1)
                dve.tensor_tensor(cmp_a, col, row, ALU.is_gt)
                step(dve.tensor_tensor(cmp_b, col, row, ALU.is_equal))
                step(dve.tensor_tensor(cmp_b, cmp_b, earlier.broadcast_to([P, NT, NE, NE]), ALU.mult))
                step(dve.tensor_tensor(cmp_a, cmp_a, cmp_b, ALU.add))
                ahead = hid[:, 0, 0:NT * NE].rearrange("p (i e) -> p i e", e=NE)
                step(dve.tensor_reduce(ahead, cmp_a, AX.X, ALU.add))
                step(dve.tensor_scalar(ahead, ahead, float(NR) - 0.5, None, ALU.is_lt))
                dve.tensor_tensor(lg[:, :, :], lg[:, :, :], mxl[:, :].unsqueeze(2).broadcast_to([P, NT, NE]),
                                  ALU.subtract).then_inc(logits_max, 1)
                dve.wait_ge(exp_ready, 1)
                step(dve.tensor_tensor(pw[:, :, :], pw[:, :, :], ahead, ALU.mult))
                step(dve.tensor_reduce(sm[:, :], pw[:, :, :], AX.X, ALU.add))
                step(dve.reciprocal(sm[:, :], sm[:, :]))
                step(dve.tensor_tensor(pw[:, :, :], pw[:, :, :], sm[:, :].unsqueeze(2).broadcast_to([P, NT, NE]),
                                       ALU.mult))
                dve.memset(pw[:, :, NR:NR + 1], 1.0).then_inc(probs_ready, 1)
                dve.wait_ge(wt_ps, 1)
                for q in range(4):
                    last = dve.tensor_copy(wt[:, q * FT:(q + 1) * FT], ps[0:NE, 4 + q, :])
                last.then_inc(wt_ready, 1)
                dve.wait_ge(wt_ready, 1)
                dve.wait_ge(w_in, 16 * 5)
                with dve.Fori(0, FN, 1) as s:
                    dve.wait_ge(acc_ps, s + 1)
                    dve.tensor_copy(wts[:, :], wt[:, bass.ds(s * FT, FT)]).then_inc(wts_ready, 1)
                    dve.wait_ge(bcast_ready, s * NR + NR)
                    for u in range(NR * HC):
                        n, c = units[u]
                        b = u % 2
                        dve.wait_ge(up_ps[b], s * per_slot + (u // 2 + 1))
                        dve.wait_ge(gate_ready[b], s * NR + (u // 2 + 1))
                        dve.scalar_tensor_tensor(act_g[:, b, :], ps[:, 2 * b + 1, :], bu[:, n * HC + c:n * HC + c + 1],
                                                 act_g[:, b, :], ALU.add, ALU.mult).then_inc(step_read, 1)
                        dve.wait_ge(step_read, s * NR * HC + (u + 1))
                        dve.wait_ge(hid_read[b], s * per_slot + 1 + u // 2)
                        dve.tensor_tensor(hid[:, b, :], act_g[:, b, :], wb[:, n, :], ALU.mult).then_inc(hid_ready[b], 1)
                    dve.wait_ge(acc_ps, s + 2)
                    for i in range(4):
                        dve.tensor_tensor(x_sb[:, s * 4 + i, :], ps[:, 4 + i, :], x_sb[:, s * 4 + i, :],
                                          ALU.add).then_inc(acc_read, 1)


def delta_stage(nc, x_in, x_out, xnt_dram, ps, cst, d):
    with ExitStack() as c2:
        sem = c2.enter_context(stage_semaphores(nc))
        sb = lambda n, s: c2.enter_context(nc.sbuf_tensor("dl_" + n, s, F32))
        xt = sb("xt", [P, KC, TT])
        state = sb("state", [P, H, P])
        wab = sb("wab", [P, KC, 2 * P + H])
        wfb = sb("wfb", [P, H * P])
        wgb = sb("wgb", [P, H * P])
        wqkv = sb("wqkv", [P, 2, 3, KC, P])
        par = sb("par", [P, H, 17])
        nega = sb("nega", [P, H])
        onw = sb("onw", [P, 1])
        kq = sb("kq", [P, 2, NG, HJ, C])
        kk = sb("kk", [P, NG, HJ, C])
        dec = sb("dec", [P, NG, HJ, C])
        val = sb("val", [P, NG, P])
        amat = sb("amat", [P, NG, 2, C])
        bdt = sb("bdt", [P, NG, HJ, C])
        bda = sb("bda", [P, NG, HJ, C])
        halo = sb("halo", [P, H, 3, 3])
        tot = sb("tot", [P, NG, HJ])
        kap = sb("kap", [P, 2 * NG])
        nkap = sb("nkap", [P, NG])
        oss = sb("oss", [P, NG])
        ofac = sb("ofac", [P, NG])
        fg = sb("fg", [P, 2, TT])
        beta = sb("beta", [H, TT])
        kapt = sb("kapt", [GH, 2, P])
        kb = sb("kb", [P, C])
        bb = sb("bb", [P, C])
        rbuf = sb("rbuf", [P, 2, P])
        ubuf = sb("ubuf", [P, 2, P])
        junk = sb("junk", [P, 2, P])
        waited = sb("waited", [P, HG + 3 * LEVELS1])
        ubd = sb("ubd", [P, HJ, P])
        tmp = sb("tmp", [P, 7188])
        raw = [tmp[:, b * 778:b * 778 + 777].rearrange("p (a t) -> p a t", a=3) for b in range(2)]
        cv = [tmp[:, 1556 + b * 768:1556 + (b + 1) * 768].rearrange("p (a t) -> p a t", a=3) for b in range(2)]
        vt = tmp[:, 3092:4116].rearrange("p (c j t) -> p c j t", j=HJ, t=C)
        sq = tmp[:, 4116:6164].rearrange("p (w c j t) -> p w c j t", w=2, j=HJ, t=C)
        sp_w, sp_ln = (kq[:, 0, n:n + NC_].rearrange("p g j t -> p (g j t)") for n in (2 * NC_, 3 * NC_))
        sp_poly = tmp[:, 6164:7188]
        nm, zm, zt = (tmp[:, n * 1024:(n + 1) * 1024].rearrange("p (s t) -> p s t", s=C) for n in range(3))
        xio = tmp[:, 2048:3072].rearrange("p (n d) -> p n d", n=2)
        sg = [tmp[:, n:n + HJ * TT].rearrange("p (h t) -> p h t", h=HJ) for n in (3072, 6164)]
        wo = [tmp[:, 4116 + n * 1024:4116 + (n + 1) * 1024].rearrange("p (h n) -> p h n", h=2) for n in range(2)]
        kkt = dec[:].rearrange("p g j t -> p g (j t)")
        ot = kk[:].rearrange("p g j t -> p (g j t)").rearrange("p (h t) -> p h t", h=H)
        by_head = lambda ap, h: ap[:, h // HJ * NC_:(h // HJ + 1) * NC_, h % HJ, :]
        by_group = lambda ap, hg: ap[:, hg * NC_:(hg + 1) * NC_].rearrange("p c j t -> p (c j t)")
        chunks = lambda ap: ap.rearrange("p (c t) -> p c t", t=C)
        kap_half = lambda hf: kap[:, :].rearrange("p (w g) -> p w g", w=2)[:, :, GH * hf:GH * hf + GH]
        sums = ps[:, 6, 0:2 * NG].rearrange("p (w g) -> p w g", w=2)
        step_group = lambda n: (n // GH * 2 + n % 2) * NC_ + n % GH // 2
        heads_state = lambda n: state[:, HJ * (n // GH * 2 + n % 2):HJ * (n // GH * 2 + n % 2) + HJ, :]
        turn_bank = lambda hg, cc: 4 if hg < 2 else (4, 0, 1, 2)[2 * (hg - 2) + cc]

        a_dram = nc.dram_tensor("akk_blocks", [HG, NC_, HJ, C, C], F32).ap()
        t_dram = nc.dram_tensor("t_blocks", [HG, NC_, HJ, C, C], F32).ap()
        k_dram = nc.dram_tensor("inverse_norms", [NG, P], F32).ap()
        b_dram = nc.dram_tensor("betas", [HG, NC_, HJ, C], F32).ap()
        ident = cst[:, K_ID:K_ID + P]

        names = """wab_in par_in wfb_in wgb_in const_ready xt_in fg_ps fg_ready beta_ps beta_ready beta_out beta_in halo_in halo_out proj_ps
            proj_read conv_done silu_done squared v_ps v_rows sums_ps roots_ready kap_ready kapt_ps kapt_ready
            sp_log sp_sum decay_ready la_ps la_done lb_ps lb_done t_ready bda_ready kkt_ps
            kkt_read tot_ready kps qps r_ready u_ps u_ready ubd_ready o_ps o_read s_ps s_read ofac_var ofac_std
            o_scaled gate_ps gate_ready ot_ps ot_ready y_ps y_ready x_loaded x_stored unit_in dve_order act_order
            pool_order""".split()
        s = {n: sem("dl_" + n) for n in names}
        pair = lambda n: [sem(f"dl_{n}{b}") for b in range(2)]
        w_in, wo_in = pair("w_in"), pair("wo_in")
        kapt_out, kapt_in, a_out, a_in = pair("kapt_out"), pair("kapt_in"), pair("a_out"), pair("a_in")
        t_out, t_in = pair("t_out"), pair("t_in")

        with nc.Block() as block:

            @block.sync
            def _(sp):
                sp.dma_start(wab[:], d["dwa"]).then_inc(s["wab_in"], 16)
                sp.dma_start(par[:], d["dheads"]).then_inc(s["par_in"], 16)
                sp.dma_start(onw[:], d["donorm"]).then_inc(s["x_stored"], 16)
                sp.wait_ge(s["x_stored"], 16)
                sp.dma_start(xt[:, :, :], xnt_dram[0]).then_inc(s["xt_in"], 16)
                for h in range(2):
                    sp.dma_start(wqkv[:, h], d["dw_qkv"][h]).then_inc(w_in[h], 16)
                    sp.dma_start(*((wfb[:], d["dwfb"]), (wgb[:], d["dwgb"]))[h]).then_inc((s["wfb_in"], s["wgb_in"])[h], 16)

                with sp.Fori(0, TN, 1) as i:
                    def inverse_norms(hf):
                        gs = slice(GH * hf, GH * hf + GH)
                        sp.wait_ge(s["kapt_ready"], i * 2 + (hf + 1))
                        sp.dma_start(k_dram[gs], kapt[:, hf, :]).then_inc(kapt_out[hf], 16)
                        sp.wait_ge(kapt_out[hf], (i + 1) * 16)
                        sp.dma_start(kb[64 * hf:64 * hf + 64, :],
                                     k_dram.rearrange("g (j t) -> (g j) t", t=C)[64 * hf:64 * hf + 64]
                                     ).then_inc(kapt_in[hf], 16)

                    def solved(hf):
                        sp.wait_ge(s["t_ready"], i * 2 + (hf + 1))
                        sp.dma_start(t_dram.rearrange("g c j s t -> (g c j) s t")[64 * hf:64 * hf + 64],
                                     zm[64 * hf:64 * hf + 64]).then_inc(t_out[hf], 16)
                        sp.wait_ge(t_out[hf], (i + 1) * 16)
                        for j in range(HJ):
                            sp.dma_start(bdt[C * j:C * j + C, GH * hf:GH * hf + GH, j, :],
                                         t_dram.rearrange("g c j s t -> j s (g c) t")[j][:, GH * hf:GH * hf + GH, :]
                                         ).then_inc(t_in[hf], 16)

                    for h in range(2, H):
                        sp.wait_ge(s["proj_ps"], i * H + (h - 1))
                        sp.dma_start(wqkv[:, h % 2], d["dw_qkv"][h]).then_inc(w_in[h % 2], 16)
                        if h == 5:
                            sp.wait_ge(s["beta_ready"], i + 1)
                            for hg in range(HG):
                                sp.dma_start(b_dram[hg].rearrange("c j t -> j c t"),
                                             beta[HJ * hg:HJ * hg + HJ, :].rearrange("j (c t) -> j c t", t=C)
                                             ).then_inc(s["beta_out"], 16)
                            sp.wait_ge(s["beta_out"], (i + 1) * 16 * HG)
                            sp.dma_start(bb[:, :], b_dram.rearrange("g c j t -> (g c j) t")).then_inc(s["beta_in"], 16)
                    inverse_norms(0)
                    for h in range(2):
                        sp.wait_ge(s["proj_ps"], i * H + (H - 1 + h))
                        sp.dma_start(wqkv[:, h], d["dw_qkv"][h]).then_inc(w_in[h], 16)
                    sp.dma_start(xt[:, :, :], xnt_dram[i + 1]).then_inc(s["xt_in"], 16)
                    sp.wait_ge(s["conv_done"], (i + 1) * H)
                    sp.wait_ge(s["halo_out"], (i + 1) * H)
                    sp.wait_ge(s["silu_done"], (i + 1) * H)
                    sp.dma_start(zm, d["unit"]).then_inc(s["unit_in"], 16)
                    sp.wait_ge(s["la_done"], (i + 1) * LEVELS1)
                    for j in range(HJ):
                        sp.dma_start(a_dram.rearrange("g c j s t -> j s (g c) t")[j][:, 0:GH, :],
                                     amat[C * j:C * j + C, 0:GH, 0, :]).then_inc(a_out[0], 16)
                    sp.wait_ge(a_out[0], (i + 1) * 16 * HJ)
                    sp.dma_start(nm[0:64], a_dram.rearrange("g c j s t -> (g c j) s t")[0:64]).then_inc(a_in[0], 16)
                    sp.wait_ge(s["sums_ps"], (i + 1) * HG)
                    for n in range(2):
                        sp.dma_start(wo[n], d["dwo"][n]).then_inc(wo_in[n], 16)
                    inverse_norms(1)
                    solved(0)
                    solved(1)
                    for n in range(2):
                        sp.dma_start(xio[:, n, :], x_in[bass.ds(i * TT + n * P, P), :]).then_inc(s["x_loaded"], 16)
                    for n in range(2, H // 2):
                        sp.wait_ge(s["y_ps"], i * (H // 2) + (n - 1))
                        sp.dma_start(wo[n % 2], d["dwo"][n]).then_inc(wo_in[n % 2], 16)
                    sp.wait_ge(s["y_ready"], i * 2 + 3)
                    for n in range(2):
                        sp.dma_start(x_out[bass.ds(i * TT + n * P, P), :], xio[:, n, :]).then_inc(s["x_stored"], 16)
                sp.wait_ge(s["x_stored"], TN * 32 + 16)
                sp.wait_ge(s["xt_in"], (TN + 1) * 16)
                for h in range(2):
                    sp.wait_ge(w_in[h], (TN * (H // 2) + 1) * 16)

            @block.gpsimd
            def _(pool):
                pool.memset(halo[:], 0.0)
                pool.memset(bdt[:], 0.0)
                pool.memset(bda[:], 0.0)
                pool.memset(ubd[:], 0.0)
                pool.memset(amat[:], 0.0).then_inc(s["const_ready"], 1)
                with pool.Fori(0, TN, 1) as i:
                    pool.wait_ge(s["y_ready"], i * 2 + 1)
                    o = Order(pool, s["pool_order"], i * POOL_PER_STEP)
                    ones = cst[:, K_ONE:K_ONE + 1].unsqueeze(2).broadcast_to([P, 3, 3])

                    def halo_in(h):
                        if h >= 2:
                            pool.wait_ge(s["conv_done"], i * H + (h - 1))
                            pool.wait_ge(s["halo_out"], i * H + (h - 1))
                        pool.tensor_tensor(raw[h % 2][:, :, 0:3], halo[:, h], ones, ALU.mult).then_inc(s["halo_in"], 1)

                    def square(h):
                        j = h % HJ
                        pool.wait_ge(s["silu_done"], i * H + (h + 1))
                        if j == 0 and h > 0:
                            pool.wait_ge(s["sums_ps"], i * HG + h // HJ)
                        k_, q_ = by_head(kk, h), by_head(kq[:, 1], h)
                        pool.tensor_tensor(sq[:, 0, :, j, :], k_, k_, ALU.mult)
                        pool.tensor_tensor(sq[:, 1, :, j, :], q_, q_, ALU.mult).then_inc(s["squared"], 1)

                    halo_in(0)
                    for h in range(H):
                        if h + 1 < H:
                            halo_in(h + 1)
                        pool.wait_ge(s["proj_read"], i * H + (h + 1))
                        pool.wait_ge(s["halo_in"], i * H + (h + 1))
                        tail = raw[h % 2][:, :, TT:TT + 3]
                        pool.tensor_tensor(halo[:, h], tail, ones, ALU.mult).then_inc(s["halo_out"], 1)
                        if h >= 1:
                            square(h - 1)
                    square(H - 1)
                    pool.wait_ge(s["squared"], (i + 1) * H)
                    for hf in range(2):
                        gs, rows = slice(GH * hf, GH * hf + GH), slice(64 * hf, 64 * hf + 64)
                        if hf == 0:
                            pool.wait_ge(s["la_done"], (i + 1) * LEVELS1)
                        else:
                            pool.wait_ge(s["lb_done"], (i + 1) * 2 * LEVELS1)
                        pool.wait_ge(s["kap_ready"], i * 2 + (hf + 1))
                        if hf == 1:
                            pool.wait_ge(s["t_ready"], i * 2 + 1)
                        for j in range(HJ):
                            q = slice(C * j, C * j + C)
                            last = pool.tensor_tensor(bda[q, gs, j, :], amat[q, gs, 1, :],
                                                      kap[q, gs].unsqueeze(2).broadcast_to([C, GH, C]), ALU.mult)
                        last.then_inc(s["bda_ready"], 1)
                        pool.wait_ge(s["bda_ready"], i * 2 + (hf + 1))
                        block_ = [64, C, C]
                        z, n_, zt_, k_, b_ = zm[rows], nm[rows], zt[rows], kb[rows], bb[rows]
                        pool.wait_ge(s["beta_in"], (i + 1) * 16)
                        pool.wait_ge(s["unit_in"], (i + 1) * 16)
                        pool.wait_ge(kapt_in[hf], (i + 1) * 16)
                        o.done(pool.tensor_tensor(z, z, b_.unsqueeze(2).broadcast_to(block_), ALU.mult))
                        o.wait()
                        o.done(pool.tensor_tensor(b_, k_, b_, ALU.mult))
                        pool.wait_ge(a_in[hf], (i + 1) * 16)
                        o.wait()
                        o.done(pool.tensor_tensor(n_, n_, k_.unsqueeze(2).broadcast_to(block_), ALU.mult))
                        o.wait()
                        o.done(pool.tensor_tensor(n_, n_, b_.unsqueeze(1).broadcast_to(block_), ALU.mult))
                        for r in range(C - 1):
                            part = [64, r + 1, C - 1 - r]
                            o.wait()
                            o.done(pool.tensor_tensor(zt_[:, 0:r + 1, r + 1:C], z[:, 0:r + 1, r:r + 1].broadcast_to(part),
                                                      n_[:, r:r + 1, r + 1:C].broadcast_to(part), ALU.mult))
                            o.wait()
                            ins = pool.tensor_tensor(z[:, 0:r + 1, r + 1:C], z[:, 0:r + 1, r + 1:C],
                                                     zt_[:, 0:r + 1, r + 1:C], ALU.subtract)
                            if r < C - 2:
                                o.done(ins)
                            else:
                                ins.then_inc(s["t_ready"], 1)
                    assert o.n == POOL_PER_STEP, o.n

            @block.scalar
            def _(act):
                act.wait_ge(s["par_in"], 16)
                act.activation(nega[:, :], par[:, :, 16], ACT.Exp).then_inc(s["act_order"], 1)
                act.wait_ge(s["act_order"], 1)
                act.activation(nega[:, :], nega[:, :], ACT.Copy, scale=-1.0).then_inc(s["act_order"], 1)
                act.wait_ge(s["act_order"], 2)
                with act.Fori(0, TN, 1) as i:
                    act.wait_ge(s["y_ready"], i * 2 + 1)
                    act.wait_ge(s["x_stored"], i * 32 + 16)
                    act.wait_ge(s["fg_ps"], (i + 1) * 2)
                    act.activation(fg[:, :, :], ps[:, 4, :].rearrange("p (a t) -> p a t", a=2),
                                   ACT.Copy).then_inc(s["fg_ready"], 1)
                    act.wait_ge(s["beta_ps"], i + 1)
                    act.activation(beta[:, :], ps[0:H, 7, 0:TT], ACT.Sigmoid).then_inc(s["beta_ready"], 1)

                    def silu(h):
                        j = h % HJ
                        act.wait_ge(s["conv_done"], i * H + (h + 1))
                        if j == 0 and h > 0:
                            act.wait_ge(s["v_ps"], i * HG + h // HJ)
                        act.activation(by_head(kq[:, 1], h), chunks(cv[h % 2][:, 0]), ACT.Silu)
                        act.activation(by_head(kk, h), chunks(cv[h % 2][:, 1]), ACT.Silu)
                        act.activation(vt[:, :, j, :], chunks(cv[h % 2][:, 2]), ACT.Silu).then_inc(s["silu_done"], 1)

                    def v_rows(hg):
                        act.wait_ge(s["v_ps"], i * HG + (hg + 1))
                        for n in range(2):
                            g0 = hg * NC_ + n * 4
                            last = act.activation(val[:, g0:g0 + 4, :], ps[:, 4 + n, :].rearrange("p (c v) -> p c v", c=4),
                                                  ACT.Copy)
                        last.then_inc(s["v_rows"], 1)

                    def softplus(hg):
                        lo = Order(act, s["sp_log"], i * 3 * HG)
                        lo.n = 3 * hg
                        if hg > 0:
                            act.wait_ge(s["sp_sum"], i * HG + hg)
                        act.wait_ge(s["proj_read"], i * H + (HJ * hg + HJ))
                        lo.done(act.activation(sp_w, by_group(dec, hg), ACT.Abs))
                        lo.wait()
                        lo.done(act.activation(sp_w, sp_w, ACT.Exp, scale=-1.0))
                        lo.wait()
                        lo.done(act.activation(sp_ln, sp_w, ACT.Ln, bias=cst[:, K_ONE:K_ONE + 1]))

                    def decay(hg):
                        act.wait_ge(s["sp_sum"], i * HG + (hg + 1))
                        for h in range(HJ * hg, HJ * hg + HJ):
                            last = act.activation(by_head(dec, h), by_head(dec, h), ACT.Exp, scale=nega[:, h:h + 1])
                        last.then_inc(s["decay_ready"], 1)

                    def roots(hf):
                        act.wait_ge(s["sums_ps"], i * HG + 2 * (hf + 1))
                        act.activation(kap_half(hf), sums[:, :, GH * hf:GH * hf + GH], ACT.Sqrt,
                                       bias=cst[:, K_EPS6:K_EPS6 + 1]).then_inc(s["roots_ready"], 1)

                    def norms_by_group(hf):
                        act.wait_ge(s["kapt_ps"], i * 2 + (hf + 1))
                        act.activation(kapt[:, hf, :], ps[0:GH, 6, P:2 * P], ACT.Copy).then_inc(s["kapt_ready"], 1)

                    def late_keys(hf):
                        act.wait_ge(s["tot_ready"], i * 2 + (hf + 1))
                        act.wait_ge(s["kap_ready"], i * 2 + (hf + 1))
                        for n in range(4):
                            act.wait_ge(s["kkt_ps"], i * 8 + (4 * hf + n + 1))
                            for m in range(4):
                                g = GH * hf + 4 * n + m
                                last = act.activation(kkt[:, g, :], ps[:, KKT_BANK[hf][n], m * P:(m + 1) * P], ACT.Copy,
                                                      scale=kap[:, g:g + 1])
                            last.then_inc(s["kkt_read"], 1)

                    def gate(hg, u):
                        act.wait_ge(s["gate_ps"], i * 8 + (2 * hg + u + 1))
                        if hg >= 2:
                            act.wait_ge(s["ot_ready"], i * 8 + (2 * hg - 2))
                        act.activation(sg[hg % 2][:, 2 * u:2 * u + 2, :], ps[:, 4, :].rearrange("p (h t) -> p h t", h=2),
                                       ACT.Sigmoid).then_inc(s["gate_ready"], 1)

                    def recurrence(hf):
                        for m in range(GH + 1):
                            n = GH * hf + m
                            if m < GH:
                                act.wait_ge(s["u_ps"], i * NG + (n + 1))
                                for j in range(HJ):
                                    q = slice(C * j, C * j + C)
                                    last = act.activation(ubd[q, j, :], ps[q, 1, 0:P], ACT.Copy)
                                last.then_inc(s["ubd_ready"], 1)
                                if n >= 2:
                                    act.wait_ge(s["o_ps"], i * NG + (n - 1))
                                act.activation(ubuf[:, m % 2, :], ps[:, 1, 0:P], ACT.Copy).then_inc(s["u_ready"], 1)
                            if m >= 1:
                                g, k = step_group(n - 1), n - 1
                                act.wait_ge(s["o_ps"], i * NG + (k + 1))
                                act.activation(val[:, g, :], ps[:, O_BANK[(m - 1) % 2], 0:P], ACT.Copy)
                                if k >= 2:
                                    act.wait_ge(s["o_read"], i * NG + (k - 1))
                                act.activation(junk[:, k % 2, :], ps[:, O_BANK[(m - 1) % 2], 0:P], ACT.Square,
                                               accum_out=oss[:, g:g + 1]).then_inc(s["o_read"], 1)
                            if hf == 1 and m >= 3 and m - 3 < len(PARTS) and PARTS[m - 3][0] == "gate":
                                gate(*PARTS[m - 3][1:])

                    def o_root(hf):
                        act.wait_ge(s["ofac_var"], i * 2 + (hf + 1))
                        f = ofac[:, GH * hf:GH * hf + GH]
                        act.activation(f, f, ACT.Sqrt, bias=cst[:, K_EPS5:K_EPS5 + 1]).then_inc(s["ofac_std"], 1)

                    for h in range(H):
                        b = h % 2
                        act.wait_ge(s["proj_ps"], i * H + (h + 1))
                        if h >= 2:
                            act.wait_ge(s["conv_done"], i * H + (h - 1))
                            act.wait_ge(s["halo_out"], i * H + (h - 1))
                            act.wait_ge(s["silu_done"], i * H + (h - 1))
                        act.activation(raw[b][:, 0:2, 3:3 + TT], ps[:, 2 * b, :].rearrange("p (a t) -> p a t", a=2), ACT.Copy)
                        act.activation(raw[b][:, 2, 3:3 + TT], ps[:, 2 * b + 1, 0:TT], ACT.Copy)
                        for a in range(3):
                            act.activation(cv[b][:, a], ps[:, 2 * b + a // 2, (a % 2) * TT:(a % 2 + 1) * TT], ACT.Identity,
                                           bias=par[:, h, 12 + a:13 + a], scale=par[:, h, 4 * a + 3:4 * a + 4])
                        act.activation(by_head(dec, h), chunks(ps[:, 2 * b + 1, TT:2 * TT]), ACT.Identity,
                                       bias=par[:, h, 15:16]).then_inc(s["proj_read"], 1)
                        if h >= 1:
                            silu(h - 1)
                        if h % HJ == 0 and h > 0:
                            softplus(h // HJ - 1)
                        if h % HJ == 2 and h > HJ:
                            decay((h - 6) // HJ)
                            v_rows((h - 6) // HJ)
                        if h == 11:
                            roots(0)
                        if h == 15:
                            norms_by_group(0)
                    silu(H - 1)
                    softplus(HG - 1)
                    v_rows(HG - 1)
                    late_keys(0)
                    decay(HG - 1)
                    roots(1)
                    for u in range(4):
                        gate(u // 2, u % 2)
                    norms_by_group(1)
                    act.wait_ge(s["lb_done"], (i + 1) * 2 * LEVELS1)
                    for j in range(HJ):
                        act.dma_start(a_dram.rearrange("g c j s t -> j s (g c) t")[j][:, GH:NG, :],
                                      amat[C * j:C * j + C, GH:NG, 0, :]).then_inc(a_out[1], 16)
                    late_keys(1)
                    act.wait_ge(a_out[1], (i + 1) * 16 * HJ)
                    act.dma_start(nm[64:128], a_dram.rearrange("g c j s t -> (g c j) s t")[64:128]).then_inc(a_in[1], 16)
                    recurrence(0)
                    o_root(0)
                    recurrence(1)
                    o_root(1)

            @block.vector
            def _(dve):
                dve.wait_ge(s["const_ready"], 1)
                dve.memset(state[:], 0.0).then_inc(s["y_ready"], 1)

                def carry(col):
                    dve.tensor_tensor(waited[:, col:col + 1], cst[:, K_ONE:K_ONE + 1], cst[:, K_ONE:K_ONE + 1], ALU.mult)

                with dve.Fori(0, TN, 1) as i:
                    o = Order(dve, s["dve_order"], i * DVE_PER_STEP)
                    dve.wait_ge(s["y_ready"], i * 2 + 1)

                    def convolve(h):
                        b = h % 2
                        dve.wait_ge(s["proj_read"], i * H + (h + 1))
                        dve.wait_ge(s["halo_in"], i * H + (h + 1))
                        for tap in range(3):
                            for a in range(3):
                                if tap > 0:
                                    o.wait(o.n - 2)
                                ins = dve.scalar_tensor_tensor(cv[b][:, a], raw[b][:, a, tap:tap + TT],
                                                               par[:, h, 4 * a + tap:4 * a + tap + 1], cv[b][:, a],
                                                               ALU.mult, ALU.add)
                                if tap == 2 and a == 2:
                                    ins.then_inc(s["conv_done"], 1)
                                else:
                                    o.done(ins)

                    def series(hg):
                        dve.wait_ge(s["sp_log"], i * 3 * HG + (3 * hg + 2))
                        o.done(dve.tensor_scalar(sp_poly, sp_w, -0.25, None, ALU.mult))
                        for c in (1.0 / 3.0, -0.5, 1.0):
                            o.wait()
                            o.done(dve.scalar_tensor_tensor(sp_poly, sp_poly, c, sp_w, ALU.add, ALU.mult))

                    def softplus(hg):
                        o.wait()
                        dve.wait_ge(s["sp_log"], i * 3 * HG + (3 * hg + 3))
                        o.done(dve.tensor_scalar(sp_w, sp_w, 2.0 ** -6, None, ALU.is_lt))
                        o.wait()
                        carry(hg)
                        o.done(dve.copy_predicated(sp_ln, sp_w.bitcast(I32), sp_poly))
                        o.wait()
                        dve.scalar_tensor_tensor(by_group(dec, hg), by_group(dec, hg), 0.0, sp_ln,
                                                 ALU.max, ALU.add).then_inc(s["sp_sum"], 1)

                    def level(lv, g0, g1, bank, ready, done, last_done, col):
                        gs, ng = slice(g0, g1), g1 - g0
                        dve.wait_ge(*ready)
                        carry(col)
                        if lv == 0:
                            mask = cst[:, K_MASK:K_MASK + C].bitcast(I32).unsqueeze(1).broadcast_to([P, ng, C])
                            dve.copy_predicated(amat[:, gs, 1, :], mask,
                                                ps[:, bank, 0:ng * C].rearrange("p (g t) -> p g t", t=C))
                            dve.wait_ge(s["decay_ready"], i * HG + (2 if g0 < GH else 4))
                            dve.tensor_tensor(kq[:, 0, gs], kk[:, gs], dec[:, gs], ALU.mult)
                            dve.tensor_tensor(kq[:, 1, gs], kq[:, 1, gs], dec[:, gs], ALU.mult).then_inc(done, 1)
                            return
                        m = 1 << (lv - 1)
                        seg = C // (2 * m)
                        view = amat[:, gs, :, :].rearrange("p g w (e r m) -> p (g w) e r m", r=2, m=m)[:, :, :, 1, :]
                        mask = cst[:, K_MASK + 32 * lv:K_MASK + 32 * lv + C // 2].bitcast(I32).rearrange(
                            "p (e m) -> p e m", m=m).unsqueeze(1).broadcast_to([P, 2 * ng, seg, m])
                        dve.copy_predicated(view, mask, ps[:, bank, 0:ng * C].rearrange("p (g e m) -> p g e m", e=seg, m=m))
                        nb = ng * HJ * C // (2 * m)
                        cut = lambda ap: ap.rearrange("p g j t -> p (g j t)").rearrange("p (n r m) -> p n r m", r=2, m=m)
                        kkv, dv = cut(kk[:, gs]), cut(dec[:, gs])
                        left, right = dv[:, :, 0, 0:1], dv[:, :, 1, 0:1]
                        dve.wait_ge(*last_done)
                        late = kq[:, :, gs].rearrange("p w g j t -> p w (g j t)").rearrange(
                            "p w (n r m) -> p w n r m", r=2, m=m)[:, :, :, 1, :]
                        o.done(dve.tensor_tensor(late, late, left.unsqueeze(1).broadcast_to([P, 2, nb, m]), ALU.mult))
                        early = kkv[:, :, 0, :]
                        o.done(dve.tensor_tensor(early, early, right.broadcast_to([P, nb, m]), ALU.mult))
                        o.wait()
                        dve.tensor_tensor(left, left, right, ALU.mult).then_inc(done, 1)

                    def level_a(lv):
                        level(lv, 0, GH, 7, (s["la_ps"], i * LEVELS1 + (lv + 1)), s["la_done"],
                              (s["la_done"], i * LEVELS1 + max(lv, 1)), HG + lv)

                    def level_b(lv, q):
                        u = 2 * lv + q
                        level(lv, GH + NC_ * q, GH + NC_ * q + NC_, L_BANK[q], (s["lb_ps"], i * 2 * LEVELS1 + (u + 1)),
                              s["lb_done"], (s["lb_done"], i * 2 * LEVELS1 + max(u - 1, 1)), HG + LEVELS1 + u)

                    def inverse_norms(hf):
                        dve.wait_ge(s["roots_ready"], i * 2 + (hf + 1))
                        o.done(dve.reciprocal(kap_half(hf), kap_half(hf)))
                        o.wait()
                        gs = slice(GH * hf, GH * hf + GH)
                        dve.tensor_scalar(nkap[:, gs], kap[:, gs], -1.0, None, ALU.mult).then_inc(s["kap_ready"], 1)

                    def whole_decay(hf):
                        gs = slice(GH * hf, GH * hf + GH)
                        dve.tensor_copy(tot[:, gs, :], dec[:, gs, :, 0]).then_inc(s["tot_ready"], 1)

                    def o_factor(hf):
                        gs = slice(GH * hf, GH * hf + GH)
                        kapq, f = kap[:, NG + GH * hf:NG + GH * hf + GH], ofac[:, gs]
                        dve.wait_ge(s["o_read"], i * NG + GH * (hf + 1))
                        o.done(dve.tensor_tensor(f, oss[:, gs], kapq, ALU.mult))
                        o.wait()
                        dve.scalar_tensor_tensor(f, f, 1.0 / (P * P), kapq, ALU.mult, ALU.mult).then_inc(s["ofac_var"], 1)

                    def o_scale(hf):
                        gs = slice(GH * hf, GH * hf + GH)
                        kapq, f = kap[:, NG + GH * hf:NG + GH * hf + GH], ofac[:, gs]
                        dve.wait_ge(s["ofac_std"], i * 2 + (hf + 1))
                        o.done(dve.reciprocal(f, f))
                        o.wait()
                        o.done(dve.scalar_tensor_tensor(f, f, float(P) ** -0.5, kapq, ALU.mult, ALU.mult))
                        o.wait()
                        for hg in (2 * hf, 2 * hf + 1):
                            gs = slice(hg * NC_, (hg + 1) * NC_)
                            dve.tensor_tensor(val[:, gs, :], val[:, gs, :],
                                              ofac[:, gs].unsqueeze(2).broadcast_to([P, NC_, P]),
                                              ALU.mult).then_inc(s["o_scaled"], 1)

                    def turned(hg, cc):
                        dve.wait_ge(s["ot_ps"], i * 8 + (2 * hg + cc + 1))
                        dve.wait_ge(s["gate_ready"], i * 8 + (2 * hg + 2))
                        dve.scalar_tensor_tensor(
                            ot[:, HJ * hg:HJ * hg + HJ, cc * P:cc * P + P],
                            ps[:, turn_bank(hg, cc), :].rearrange("p (j t) -> p j t", j=HJ), onw[:, 0:1],
                            sg[hg % 2][:, :, cc * P:cc * P + P], ALU.mult, ALU.mult).then_inc(s["ot_ready"], 1)

                    def recurrence(hf):
                        decayed = {}
                        for m in range(GH + 2):
                            n = GH * hf + m
                            if m < GH:
                                g = step_group(n)
                                dve.wait_ge(s["kps"], i * NG + (n + 1))
                                if n >= 2:
                                    dve.wait_ge(s["u_ps"], i * NG + (n - 1))
                                dve.scalar_tensor_tensor(rbuf[:, m % 2, :], ps[:, 0, 0:P], nkap[:, g:g + 1], val[:, g, :],
                                                         ALU.mult, ALU.add).then_inc(s["r_ready"], 1)
                            if 1 <= m <= GH:
                                st = heads_state(n - 1)
                                dve.wait_ge(s["s_ps"], i * NG + n)
                                o.wait(decayed[m - 1])
                                dve.tensor_tensor(st, st, ps[:, 3, :].rearrange("p (h v) -> p h v", h=HJ),
                                                  ALU.add).then_inc(s["s_read"], 1)
                            if m < GH:
                                st = heads_state(n)
                                dve.wait_ge(s["qps"], i * NG + (n + 1))
                                if m >= 2:
                                    dve.wait_ge(s["s_read"], i * NG + (n - 1))
                                decayed[m] = o.done(dve.tensor_tensor(
                                    st, st, tot[:, step_group(n), :].unsqueeze(2).broadcast_to([P, HJ, P]), ALU.mult))

                    for h in range(H):
                        convolve(h)
                        if h >= 10:
                            level_a(h - 10)
                        if h % HJ == 0 and h > 0:
                            series(h // HJ - 1)
                        if h % HJ == 1 and h > 1:
                            softplus(h // HJ - 1)
                        if h == 12:
                            inverse_norms(0)
                    dve.wait_ge(s["la_done"], (i + 1) * LEVELS1)
                    whole_decay(0)
                    series(HG - 1)
                    softplus(HG - 1)
                    for lv in range(LEVELS1):
                        level_b(lv, 0)
                        level_b(lv, 1)
                        if lv == 0:
                            inverse_norms(1)
                    dve.wait_ge(s["lb_done"], (i + 1) * 2 * LEVELS1)
                    whole_decay(1)
                    dve.wait_ge(s["v_rows"], (i + 1) * HG)
                    dve.wait_ge(s["kap_ready"], i * 2 + 2)
                    dve.wait_ge(s["tot_ready"], i * 2 + 2)
                    recurrence(0)
                    o_factor(0)
                    o_scale(0)
                    for hg in (0, 1):
                        for cc in range(2):
                            turned(hg, cc)
                    recurrence(1)
                    o_factor(1)
                    o_scale(1)
                    for hg in (2, 3):
                        for cc in range(2):
                            turned(hg, cc)
                    dve.wait_ge(s["y_ps"], (i + 1) * (H // 2))
                    dve.wait_ge(s["x_loaded"], (i + 1) * 32)
                    for n in range(2):
                        dve.tensor_tensor(xio[:, n, :], ps[:, 6 + n, :], xio[:, n, :], ALU.add).then_inc(s["y_ready"], 1)
                    assert o.n == DVE_PER_STEP, o.n

            @block.tensor
            def _(pe):
                pe.wait_ge(s["wab_in"], 16)
                with pe.Fori(0, TN, 1) as i:
                    pe.wait_ge(s["y_ready"], i * 2 + 1)
                    pe.wait_ge(s["xt_in"], (i + 1) * 16)
                    for a in range(2):
                        for k in range(KC):
                            last = pe.matmul(ps[:, 4, a * TT:(a + 1) * TT], wab[:, k, a * P:(a + 1) * P], xt[:, k, :],
                                             start=(k == 0), stop=(k == KC - 1))
                        last.then_inc(s["fg_ps"], 1)
                    for k in range(KC):
                        last = pe.matmul(ps[0:H, 7, 0:TT], wab[:, k, 2 * P:2 * P + H], xt[:, k, :],
                                         start=(k == 0), stop=(k == KC - 1))
                    last.then_inc(s["beta_ps"], 1)

                    def project(h):
                        b = h % 2
                        pe.wait_ge(w_in[b], (i * (H // 2) + (h // 2 + 1)) * 16)
                        if h >= 2:
                            pe.wait_ge(s["proj_read"], i * H + (h - 1))
                        for a in range(3):
                            for k in range(KC):
                                pe.matmul(ps[:, 2 * b + a // 2, (a % 2) * TT:(a % 2 + 1) * TT], wqkv[:, b, a, k, :],
                                          xt[:, k, :], start=(k == 0), stop=(k == KC - 1))
                        if h == 0:
                            pe.wait_ge(s["wfb_in"], 16)
                            pe.wait_ge(s["fg_ready"], i + 1)
                        pe.matmul(ps[:, 2 * b + 1, TT:2 * TT], wfb[:, h * P:(h + 1) * P], fg[:, 0, :],
                                  start=True, stop=True).then_inc(s["proj_ps"], 1)

                    def group(hg):
                        pe.wait_ge(s["silu_done"], i * H + (HJ * hg + HJ))
                        if hg > 0:
                            pe.wait_ge(s["v_rows"], i * HG + hg)
                        for c in range(NC_):
                            last = pe.transpose(ps[:, 4 + c // 4, (c % 4) * P:(c % 4 + 1) * P],
                                                vt[:, c].rearrange("p j t -> p (j t)"), ident)
                        last.then_inc(s["v_ps"], 1)
                        pe.wait_ge(s["squared"], i * H + (HJ * hg + HJ))
                        if hg == 2:
                            pe.wait_ge(s["roots_ready"], i * 2 + 1)
                        if hg == 3:
                            pe.wait_ge(s["kapt_ready"], i * 2 + 1)
                        for w in range(2):
                            for c in range(NC_):
                                col = w * NG + hg * NC_ + c
                                last = pe.matmul(ps[:, 6, col:col + 1], sq[:, w, c].rearrange("p j t -> p (j t)"),
                                                 cst[:, K_ONE:K_ONE + 1], start=True, stop=True)
                        last.then_inc(s["sums_ps"], 1)

                    def level(lv, g0, g1, bank):
                        m = 1 << max(lv - 1, 0)
                        for g in range(g0, g1):
                            n = g - g0
                            for j in range(HJ):
                                if lv == 0:
                                    rhs = kq[:, 1, g, j, :]
                                else:
                                    rhs = kq[:, :, g, j, :].rearrange("p w (e r m) -> p w e r m", r=2, m=m)[:, :, :, 1, :]
                                last = pe.matmul(ps[C * j:C * j + C, bank, n * C:(n + 1) * C], kk[:, g, j, :], rhs,
                                                 start=True, stop=True)
                        return last

                    def level_a(lv):
                        if lv == 0:
                            pe.wait_ge(s["silu_done"], i * H + 8)
                            pe.wait_ge(s["beta_ready"], i + 1)
                        else:
                            pe.wait_ge(s["la_done"], i * LEVELS1 + lv)
                        level(lv, 0, GH, 7).then_inc(s["la_ps"], 1)

                    def level_b(lv, q):
                        if lv > 0:
                            pe.wait_ge(s["lb_done"], i * 2 * LEVELS1 + (2 * lv + q - 1))
                        level(lv, GH + NC_ * q, GH + NC_ * q + NC_, L_BANK[q]).then_inc(s["lb_ps"], 1)

                    def late_keys(hf):
                        for n in range(4):
                            if hf == 1 and n >= 2:
                                pe.wait_ge(s["kkt_read"], i * 8 + (4 + n - 1))
                            for m in range(4):
                                g = GH * hf + 4 * n + m
                                last = pe.transpose(ps[:, KKT_BANK[hf][n], m * P:(m + 1) * P],
                                                    kk[:, g].rearrange("p j t -> p (j t)"), ident)
                            last.then_inc(s["kkt_ps"], 1)

                    def norms_by_group(hf):
                        pe.wait_ge(s["kap_ready"], i * 2 + (hf + 1))
                        pe.transpose(ps[0:GH, 6, P:2 * P], kap[:, GH * hf:GH * hf + GH], ident).then_inc(s["kapt_ps"], 1)

                    def gate(hg, u):
                        if 2 * hg + u == 0:
                            pe.wait_ge(s["wgb_in"], 16)
                        if hg >= 2:
                            pe.wait_ge(s["ot_ready"], i * 8 + 4)
                        if 2 * hg + u > 0:
                            pe.wait_ge(s["gate_ready"], i * 8 + (2 * hg + u))
                        for n in range(2):
                            h = HJ * hg + 2 * u + n
                            last = pe.matmul(ps[:, 4, n * TT:(n + 1) * TT], wgb[:, h * P:(h + 1) * P], fg[:, 1, :],
                                             start=True, stop=True)
                        last.then_inc(s["gate_ps"], 1)

                    def turn(hg, cc):
                        t = 2 * hg + cc
                        pe.wait_ge(s["o_scaled"], i * HG + (hg + 1))
                        pe.wait_ge(s["gate_ready"], i * 8 + (4 if hg < 2 else 8))
                        if t > 0:
                            pe.wait_ge(s["ot_ready"], i * 8 + min(t, 4))
                        for n in range(4):
                            by_chunk = ps[:, turn_bank(hg, cc), :].rearrange("p (j c t) -> p c j t", j=HJ, t=C)
                            last = pe.transpose(by_chunk[:, n],
                                                val[:, hg * NC_ + 4 * cc + n, :], ident)
                        last.then_inc(s["ot_ps"], 1)

                    def out_rows(h):
                        if h % 2 == 0:
                            pe.wait_ge(wo_in[h // 2 % 2], (i * (H // 4) + (h // 4 + 1)) * 16)
                        pe.wait_ge(s["ot_ready"], i * 8 + (2 * (h // HJ) + 2))
                        for k in range(2):
                            last = pe.matmul(ps[:, 6 + k, :], ot[:, h, k * P:(k + 1) * P], wo[h // 2 % 2][:, h % 2, :],
                                             start=(h == 0), stop=(h == H - 1))
                        if h % 2 == 1:
                            last.then_inc(s["y_ps"], 1)

                    def recurrence(hf):
                        gs = slice(GH * hf, GH * hf + GH)
                        for m in range(GH + 2):
                            n = GH * hf + m
                            if m < GH:
                                if m >= 2:
                                    pe.wait_ge(s["s_read"], i * NG + (n - 1))
                                if n > 0:
                                    pe.wait_ge(s["r_ready"], i * NG + n)
                                g = step_group(n)
                                for j in range(HJ):
                                    last = pe.matmul(ps[C * j:C * j + C, 0, 0:P], kq[:, 0, g, j, :],
                                                     heads_state(n)[:, j, :], start=True, stop=True)
                                last.then_inc(s["kps"], 1)
                            if 1 <= m <= GH:
                                pe.wait_ge(s["ubd_ready"], i * NG + n)
                                if n >= 2:
                                    pe.wait_ge(s["s_read"], i * NG + (n - 1))
                                pe.matmul(ps[:, 3, :], kkt[:, step_group(n - 1), :], ubd[:, :, :].rearrange("p j v -> p (j v)"),
                                          start=True, stop=True).then_inc(s["s_ps"], 1)
                            if m < GH:
                                if m == 0:
                                    pe.wait_ge(t_in[hf], (i + 1) * 16 * HJ)
                                pe.wait_ge(s["r_ready"], i * NG + (n + 1))
                                if n > 0:
                                    pe.wait_ge(s["u_ready"], i * NG + n)
                                pe.matmul(ps[:, 1, 0:P], bdt[:, g].rearrange("p j t -> p (j t)"), rbuf[:, m % 2, :],
                                          start=True, stop=True).then_inc(s["u_ps"], 1)
                                if n >= 2:
                                    pe.wait_ge(s["o_read"], i * NG + (n - 1))
                                for j in range(HJ):
                                    last = pe.matmul(ps[C * j:C * j + C, O_BANK[m % 2], 0:P], kq[:, 1, g, j, :],
                                                     heads_state(n)[:, j, :], start=True, stop=False,
                                                     skip_group_check=True)
                                last.then_inc(s["qps"], 1)
                            if 1 <= m <= GH:
                                if m == 1:
                                    pe.wait_ge(s["bda_ready"], i * 2 + (hf + 1))
                                pe.wait_ge(s["u_ready"], i * NG + n)
                                pe.matmul(ps[:, O_BANK[(m - 1) % 2], 0:P],
                                          bda[:, step_group(n - 1)].rearrange("p j t -> p (j t)"), ubuf[:, (m - 1) % 2, :],
                                          start=False, stop=True, skip_group_check=True).then_inc(s["o_ps"], 1)
                            if hf == 1 and 2 <= m < len(PARTS) + 2:
                                kind, arg = PARTS[m - 2][0], PARTS[m - 2][1:]
                                if kind == "gate":
                                    gate(*arg)
                                else:
                                    out_rows(*arg)

                    for h in range(H):
                        project(h)
                        if h >= 10:
                            level_a(h - 10)
                        if h % HJ == 1 and h > HJ:
                            group((h - 5) // HJ)
                        if h == 14:
                            norms_by_group(0)
                    group(HG - 1)
                    pe.wait_ge(s["la_done"], (i + 1) * LEVELS1)
                    pe.wait_ge(s["proj_read"], (i + 1) * H)
                    late_keys(0)
                    pe.wait_ge(s["v_rows"], (i + 1) * HG)
                    for u in range(2 * LEVELS1):
                        level_b(u // 2, u % 2)
                        if u in (1, 2, 3, 4):
                            gate((u - 1) // 2, (u - 1) % 2)
                        if u == 5:
                            norms_by_group(1)
                    pe.wait_ge(s["lb_done"], (i + 1) * 2 * LEVELS1)
                    pe.wait_ge(s["gate_ready"], i * 8 + 4)
                    pe.wait_ge(s["kapt_ready"], i * 2 + 2)
                    late_keys(1)
                    pe.wait_ge(s["kkt_read"], (i + 1) * 8)
                    recurrence(0)
                    for hg in (0, 1):
                        for cc in range(2):
                            turn(hg, cc)
                    recurrence(1)
                    out_rows(6)
                    out_rows(7)
                    pe.wait_ge(s["r_ready"], (i + 1) * NG)
                    pe.wait_ge(s["u_ready"], (i + 1) * NG)
                    pe.wait_ge(s["o_read"], (i + 1) * NG)
                    for hg in (2, 3):
                        for cc in range(2):
                            turn(hg, cc)
                    for h in range(H // 2, H):
                        out_rows(h)


def program(nc, d, out, until=9):
    with ExitStack() as ctx:
        sem = lambda n: ctx.enter_context(nc.semaphore(n))
        ps = ctx.enter_context(nc.psum_tensor("psum", [P, 8, 512], F32))
        cst = ctx.enter_context(nc.sbuf_tensor("constants_sb", [P, K_N], F32))
        x1 = nc.dram_tensor("x_after_attention", [T, D], F32).ap()
        x2 = nc.dram_tensor("x_after_experts", [T, D], F32).ap()
        x3 = nc.dram_tensor("x_after_delta", [T, D], F32).ap()
        xnt_dram = nc.dram_tensor("xn_transposed", [TN + 1, P, KC, TT], F32).ap()

        def gates_weights(c2, n):
            wg = c2.enter_context(nc.sbuf_tensor(f"wgate{n}", [P, NR, KC, FH], F32))
            wu = c2.enter_context(nc.sbuf_tensor(f"wup{n}", [P, NR, KC, FH], F32))
            wgu_in = sem(f"wgu_in{n}")

            def ahead(sp):
                sp.dma_start(wg[:], d["wgate"]).then_inc(wgu_in, 16)
                sp.dma_start(wu[:], d["wup"]).then_inc(wgu_in, 16)
            return wg, wu, wgu_in, ahead

        with ExitStack() as c2:
            x_sb = c2.enter_context(nc.sbuf_tensor("x1_sb", [P, NT, D], F32))
            xnt = c2.enter_context(nc.sbuf_tensor("xnt1_sb", [P, KC, T], F32))
            wg, wu, wgu_in, ahead = gates_weights(c2, 1)
            norm_stage(nc, "n1_", x_sb, xnt, ps, cst, gram=True, source=d["x"], constants_from=d["constants"])
            attention_stage(nc, x_sb, xnt, ps, cst, d, ahead)
            norm_stage(nc, "n2_", x_sb, xnt, ps, cst)
            ffn_stage(nc, "f1_", x_sb, xnt, ps, cst, d, x2 if until > 1 else out, wg, wu, wgu_in)
            if until == 1:
                return
            norm_stage(nc, "n3_", x_sb, xnt, ps, cst, store_to=xnt_dram)
        delta_stage(nc, x2, x3 if until > 2 else out, xnt_dram, ps, cst, d)
        if until == 2:
            return
        with ExitStack() as c2:
            x_sb = c2.enter_context(nc.sbuf_tensor("x3_sb", [P, NT, D], F32))
            xnt = c2.enter_context(nc.sbuf_tensor("xnt3_sb", [P, KC, T], F32))
            wg, wu, wgu_in, ahead = gates_weights(c2, 2)
            norm_stage(nc, "n4_", x_sb, xnt, ps, cst, source=x3, ahead=ahead)
            ffn_stage(nc, "f2_", x_sb, xnt, ps, cst, d, out, wg, wu, wgu_in)


def arrange(inputs):
    import numpy as np
    f = {k.split("L0_")[1]: np.asarray(v) for k, v in inputs.items()}
    rows = lambda a, k: a.reshape(k, P, -1).transpose(1, 0, 2)
    d = {"constants": constants(), "x": f["attn_a_x"][0]}
    d["select"] = np.repeat(np.eye(NE, NR, dtype=np.float32)[:, :, None], P, 2)
    d["unit"] = np.broadcast_to(np.eye(C, dtype=np.float32), (P, C, C))
    d["wq"], d["wk"], d["wo"] = f["attn_a_Wq"], f["attn_a_Wk"], f["attn_a_Wo"]
    d["wvt"] = f["attn_a_Wv"].T
    d["router"] = rows(f["ffn_Wg"], KC)
    d["brouter"] = np.broadcast_to(f["ffn_bg"], (P, NE))
    d["wgate"] = f["ffn_Wgate"].reshape(NR, KC, P, FH).transpose(2, 0, 1, 3)
    d["wup"] = f["ffn_Wup"].reshape(NR, KC, P, FH).transpose(2, 0, 1, 3)
    d["wdown"] = f["ffn_Wdown"].reshape(NR, HC, P, D).transpose(2, 0, 1, 3)
    d["wsup"], d["wsdown"] = rows(f["ffn_Ws_up"], KC), rows(f["ffn_Ws_down"], SC)
    d["bgate"] = f["ffn_bgate"].reshape(NR * HC, P).T
    d["bup"] = f["ffn_bup"].reshape(NR * HC, P).T
    d["bsup"] = f["ffn_bs_up"].reshape(SC, P).T
    d["bdown"] = np.concatenate([f["ffn_bdown"], f["ffn_bs_down"][None]])
    heads = lambda a: a.reshape(KC, P, H, P).transpose(2, 1, 0, 3)
    d["dw_qkv"] = np.stack([heads(f["attn_b_Wq"]), heads(f["attn_b_Wk"]), heads(f["attn_b_Wv"])], 2)
    per = [f[f"attn_b_conv_{n}_w"].reshape(H, P, 4).transpose(1, 0, 2) for n in "qkv"]
    per += [f[f"attn_b_conv_{n}_b"].reshape(H, P, 1).transpose(1, 0, 2) for n in "qkv"]
    per += [f["attn_b_dt_bias"].reshape(H, P, 1).transpose(1, 0, 2)]
    per += [np.broadcast_to(f["attn_b_A_log"][None, :, None], (P, H, 1))]
    d["dheads"] = np.concatenate(per, 2)
    d["dwa"] = np.concatenate([rows(f["attn_b_Wfa"], KC), rows(f["attn_b_Wga"], KC), rows(f["attn_b_Wb"], KC)], 2)
    d["dwfb"], d["dwgb"] = f["attn_b_Wfb"], f["attn_b_Wgb"]
    d["donorm"] = f["attn_b_o_norm_w"].reshape(P, 1)
    d["dwo"] = f["attn_b_Wo"].reshape(H // 2, 2, P, D).transpose(0, 2, 1, 3)
    return {k: np.ascontiguousarray(v) for k, v in d.items()}


def kernel(**inputs):
    import numpy as np
    import concourse.bacc as bacc
    from concourse.bass_utils import run_bass_kernel_spmd

    arrays = arrange(inputs)
    nc = bacc.Bacc("TRN2", target_bir_lowering=False, num_devices=1)
    d = {n: nc.dram_tensor("in_" + n, a.shape, mybir.dt.from_np(a.dtype), kind="ExternalInput").ap()
         for n, a in arrays.items()}
    out = nc.dram_tensor("out", (T, D), F32, kind="ExternalOutput").ap()
    program(nc, d, out)
    r = run_bass_kernel_spmd(nc, [{"in_" + n: a for n, a in arrays.items()}], core_ids=[0])
    return r.results[0]["out"].reshape(1, T, D)
```
